# Optimizing a Trainium2 kernel written in Bass

```python
import numpy as np
import jax
import jax.numpy as jnp

def _softmax(x, axis=-1):
    return jax.nn.softmax(x, axis=axis)
def _gelu(x):
    return jax.nn.gelu(x, approximate=True)
def _silu(x):
    return jax.nn.silu(x)
def _sigmoid(x):
    return jax.nn.sigmoid(x)
def _layernorm(x, axis=-1, eps=1e-5):
    m = jnp.mean(x, axis=axis, keepdims=True)
    v = jnp.var(x, axis=axis, keepdims=True)
    return (x - m) / jnp.sqrt(v + eps)
def _scatter_add(tgt, idx, src, axis=0):
    return tgt.at[idx].add(src)
def _segment_sum(src, seg, n):
    return jax.ops.segment_sum(src, seg, n)

kernel_name = 'mk_conv_preact_d2_conv_nchw768_0a7936'

def setup_inputs(seed: int = 0):
    np.random.seed(seed)
    _w = jnp.asarray
    def _rec_inputs():
        import jax
        import jax.numpy as jnp
        _gk = jax.random.key(seed)
        x = -0.0004039 + 1 * jax.random.normal(jax.random.fold_in(_gk, 1), (16, 768, 32, 32), jnp.float32)
        return x
    x = _rec_inputs()
    def _L0_conv_setup():
        import jax, jax.numpy as jnp
        import numpy as np
        DIM = 768
        EPS = 1e-06

        def _layernorm(x, gamma, beta):
            mu = jnp.mean(x, axis=-1, keepdims=True)
            var = jnp.mean(jnp.square(x - mu), axis=-1, keepdims=True)
            return (x - mu) * jax.lax.rsqrt(var + EPS) * gamma + beta
        key = jax.random.key(seed)
        ks = jax.random.split(key, 10)
        B, C, H, W = (16, DIM, 32, 32)
        s = 1.0 / np.sqrt(C)
        return {'x': jax.random.normal(ks[0], (B, C, H, W), dtype=jnp.float32), 'W1': jax.random.uniform(ks[1], (C, C), jnp.float32, -s, s), 'b1': jax.random.uniform(ks[2], (C,), jnp.float32, -s, s), 'g1': jnp.ones((C,), jnp.float32), 'beta1': jnp.zeros((C,), jnp.float32), 'W2': jax.random.uniform(ks[3], (C, C), jnp.float32, -s, s), 'b2': jax.random.uniform(ks[4], (C,), jnp.float32, -s, s), 'g2': jnp.ones((C,), jnp.float32), 'beta2': jnp.zeros((C,), jnp.float32), 'W3': jax.random.uniform(ks[5], (C, C), jnp.float32, -s, s), 'b3': jax.random.uniform(ks[6], (C,), jnp.float32, -s, s)}
    _L0_conv_all = _L0_conv_setup()
    _L0_conv_in = {k: v for k, v in _L0_conv_all.items() if k in ('W1', 'b1', 'g1', 'beta1', 'W2', 'b2', 'g2', 'beta2', 'W3', 'b3', )}
    del _L0_conv_all

    def _L1_conv_setup():
        import jax, jax.numpy as jnp
        import numpy as np

        def hardsigmoid(x):
            return jnp.clip(x / 6.0 + 0.5, 0.0, 1.0)
        key = jax.random.key(seed)
        k1, k2, k3 = jax.random.split(key, 3)
        B, C, H, Wd = (32, 768, 56, 56)
        x = jax.random.normal(k1, (B, C, H, Wd), dtype=jnp.float32)
        W = jax.random.normal(k2, (C, C), dtype=jnp.float32) * (1.0 / np.sqrt(C))
        b = jax.random.normal(k3, (C,), dtype=jnp.float32) * 0.01
        return {'x': x, 'W': W, 'b': b}
    _L1_conv_all = _L1_conv_setup()
    _L1_conv_in = {k: v for k, v in _L1_conv_all.items() if k in ('W', 'b', )}
    del _L1_conv_all

    return {
        "x": x,
        "L0_conv_W1": _L0_conv_in["W1"],
        "L0_conv_b1": _L0_conv_in["b1"],
        "L0_conv_g1": _L0_conv_in["g1"],
        "L0_conv_beta1": _L0_conv_in["beta1"],
        "L0_conv_W2": _L0_conv_in["W2"],
        "L0_conv_b2": _L0_conv_in["b2"],
        "L0_conv_g2": _L0_conv_in["g2"],
        "L0_conv_beta2": _L0_conv_in["beta2"],
        "L0_conv_W3": _L0_conv_in["W3"],
        "L0_conv_b3": _L0_conv_in["b3"],
        "L1_conv_W": _L1_conv_in["W"],
        "L1_conv_b": _L1_conv_in["b"],
    }

def reference(x, L0_conv_W1, L0_conv_b1, L0_conv_g1, L0_conv_beta1, L0_conv_W2, L0_conv_b2, L0_conv_g2, L0_conv_beta2, L0_conv_W3, L0_conv_b3, L1_conv_W, L1_conv_b):
    import jax
    import jax.numpy as jnp
    def _L0_conv_ref(x, W1, b1, g1, beta1, W2, b2, g2, beta2, W3, b3):
        import jax, jax.numpy as jnp
        import numpy as np
        DIM = 768
        EPS = 1e-06

        def _layernorm(x, gamma, beta):
            mu = jnp.mean(x, axis=-1, keepdims=True)
            var = jnp.mean(jnp.square(x - mu), axis=-1, keepdims=True)
            return (x - mu) * jax.lax.rsqrt(var + EPS) * gamma + beta
        h = jnp.transpose(x, (0, 2, 3, 1))
        h = jnp.einsum('bhwc,oc->bhwo', h, W1) + b1
        h = jax.nn.gelu(_layernorm(h, g1, beta1), approximate=False)
        h = jnp.einsum('bhwc,oc->bhwo', h, W2) + b2
        h = jax.nn.gelu(_layernorm(h, g2, beta2), approximate=False)
        h = jnp.einsum('bhwc,oc->bhwo', h, W3) + b3
        return jnp.transpose(h, (0, 3, 1, 2))

    def _L1_conv_ref(x, W, b):
        import jax, jax.numpy as jnp
        import numpy as np

        def hardsigmoid(x):
            return jnp.clip(x / 6.0 + 0.5, 0.0, 1.0)
        x_se = x.mean(axis=(2, 3))
        x_se = jnp.einsum('bc,oc->bo', x_se, W) + b
        return x * hardsigmoid(x_se)[:, :, None, None]

    def _gn(v, G=32, eps=1e-5):
        B_, C_, H_, W_ = v.shape
        g = v.reshape(B_, G, C_ // G, H_, W_)
        m = jnp.mean(g, axis=(2, 3, 4), keepdims=True)
        s = jnp.var(g, axis=(2, 3, 4), keepdims=True)
        return ((g - m) / jnp.sqrt(s + eps)).reshape(v.shape)

    def _ln_c(v, eps=1e-6):
        m = jnp.mean(v, axis=1, keepdims=True)
        s = jnp.var(v, axis=1, keepdims=True)
        return (v - m) / jnp.sqrt(s + eps)

    def _ln_t(v, eps=1e-5):
        m = jnp.mean(v, axis=-1, keepdims=True)
        s = jnp.var(v, axis=-1, keepdims=True)
        return (v - m) / jnp.sqrt(s + eps)

    def _to_tokens(v):
        B_, C_, H_, W_ = v.shape
        return v.reshape(B_, C_, H_ * W_).transpose(0, 2, 1)
    def _from_tokens(t, like):
        B_, C_, H_, W_ = like.shape
        return t.transpose(0, 2, 1).reshape(B_, C_, H_, W_)

    x = x + _L0_conv_ref(_gn(x), L0_conv_W1, L0_conv_b1, L0_conv_g1, L0_conv_beta1, L0_conv_W2, L0_conv_b2, L0_conv_g2, L0_conv_beta2, L0_conv_W3, L0_conv_b3)
    x = x + _L1_conv_ref(_gn(x), L1_conv_W, L1_conv_b)
    return x


_drawn_inputs = setup_inputs


def setup_inputs(seed=0):
    import zlib

    import numpy as np

    out = dict(_drawn_inputs(seed))
    spreads = {'L0_conv_g1': (1.0, 0.2),
     'L0_conv_beta1': (0.0, 0.1),
     'L0_conv_g2': (1.0, 0.2),
     'L0_conv_beta2': (0.0, 0.1)}
    factors = {'L0_conv_b1': 4.062, 'L0_conv_b2': 2.757, 'L0_conv_b3': 2.842, 'L1_conv_b': 51.75}
    for name, (base, spread) in spreads.items():
        noise = np.random.default_rng([zlib.crc32(name.encode()), seed]).standard_normal(out[name].shape)
        drawn = base * np.exp(spread * noise) if base else spread * noise
        out[name] = jnp.asarray(drawn.astype(out[name].dtype))
    for name, factor in factors.items():
        out[name] = (out[name] * factor).astype(out[name].dtype)
    return out
```

```python
from contextlib import ExitStack
from typing import NamedTuple

import concourse.bass as bass
from concourse import mybir

F32 = mybir.dt.float32
F32R = mybir.dt.float32r
ALU = mybir.AluOpType
ACT = mybir.ActivationFunctionType
AX = mybir.AxisListType

P = 128
B, C, HW = 16, 768, 1024
T = C // P
CPG = C // 32
PPG = CPG // T
TOK = 256
TILES = HW // TOK
PAIRS = TILES // 2
LAYERS = 3
XCH = 512
XPIECES = range(T * HW // XCH)
RING = 3
EPS_LN = 1e-6
EPS_GN = 1e-5

PHASES = [(layer, 2 * pair + par, par) for pair in range(PAIRS) for layer in range(LAYERS) for par in range(2)]
NPH = len(PHASES)
LN = [k for k in range(NPH) if PHASES[k][0] < LAYERS - 1]
BANKS = T * TOK // 512
OPB = T // BANKS

PREV = ["g1", "g2", "se"]
NEXT = ["gx1", "gx2"]
SMALL = ["ln0", "g1", "g2", "ln1", "se", "ln2", "ln3", "ln4", "ln5", "ln6", "ln7", "gx1", "gx2"]
STEPS = ["y_mean", "y_spread", "z", "gate", "gain", "shift", "x_mean", "x_spread"]
PREV_STEPS = STEPS[:6]
N_SETUP_SMALL = 2 + 2


class Img(NamedTuple):
    i: object
    slot: int
    use: object
    kind: str


def small_no(im, name):
    if im.kind == "first":
        return N_SETUP_SMALL + [u for u in SMALL if u not in PREV].index(name)
    base = N_SETUP_SMALL + len(SMALL) - len(PREV) + (im.i - 1) * len(SMALL)
    if im.kind == "end":
        return base - len(NEXT) + PREV.index(name)
    return base + (SMALL if im.kind == "mid" else [u for u in SMALL if u not in NEXT]).index(name)


def step_no(im, name):
    if im.kind == "setup":
        return ["x_mean", "x_spread"].index(name) + 1
    if im.kind == "first":
        return 2 + [s for s in STEPS if s not in PREV_STEPS].index(name) + 1
    base = 2 + len(STEPS) - len(PREV_STEPS) + (im.i - 1) * len(STEPS)
    if im.kind == "end":
        base = base - (len(STEPS) - len(PREV_STEPS))
    return base + STEPS.index(name) + 1


def program(nc, x, W1, b1, g1, beta1, W2, b2, g2, beta2, W3, b3, LW, Lb, out):
    x_v = x.rearrange("b (p t) h w -> b p t (h w)", p=P)
    out_v = out.rearrange("b (p t) h w -> b p t (h w)", p=P)

    ctx = ExitStack()
    with ctx:
        def sb(name, shape, dt=F32):
            return ctx.enter_context(nc.sbuf_tensor(name, shape, dt))

        def psum(name, shape):
            return ctx.enter_context(nc.psum_tensor(name, shape, F32))

        def sem(name):
            return ctx.enter_context(nc.semaphore(name))

        h = [psum(f"h{par}", [P, T, TOK]) for par in range(2)]
        small = psum("small", [P, 512])
        bc = psum("bc", [P, 512])

        w_hi = sb("w_hi", [P, LAYERS, T, T, P], F32R)
        w_lo = sb("w_lo", [P, LAYERS, T, T, P], F32R)
        lw = sb("lw", [P, T, T, P])
        x_sb = sb("x_sb", [P, 2, T, HW])
        a_hi = sb("a_hi", [P, 2, T, TOK], F32R)
        a_lo = sb("a_lo", [P, 2, T, TOK], F32R)
        t_ring = sb("t_ring", [P, RING, TOK])
        sq = sb("sq", [P, 2, TOK])
        sqsum = sb("sqsum", [P, TOK])
        diag = sb("diag", [P, TOK])
        ident = sb("ident", [P, P])
        ones = sb("ones", [P, P])
        gmean = sb("gmean", [P, P])
        vec = sb("vec", [P, 8, T])
        bias = [vec[:, 0, :], vec[:, 1, :], vec[:, 2, :]]
        gam = [vec[:, 3, :], vec[:, 4, :]]
        bet = [vec[:, 5, :], vec[:, 6, :]]
        lbias = vec[:, 7, :]
        xstat = sb("xstat", [P, T * HW // XCH, 6])
        ystat = sb("ystat", [P, T, TILES, 6])
        scal = sb("scal", [P, 58])
        ymean = scal[:, 0:12].rearrange("p (t a) -> p t a", t=T)
        gs = scal[:, 12:28].rearrange("p (w a) -> p w a", w=2)
        lnv = scal[:, 28:30]
        lnr = scal[:, 30:32]
        mhalf = scal[:, 32:34]
        se = scal[:, 34:58].rearrange("p (w t) -> p w t", w=4)
        wmean = ystat[:].rearrange("p t a b -> p (t a b)")[:, 0:2 * T + 4]

        w_loaded = [sem(f"w_loaded{m}") for m in range(4)]
        vec_loaded = sem("vec_loaded")
        x_loaded = [sem(f"x_loaded{s}") for s in range(2)]
        stored = [sem(f"stored{s}") for s in range(2)]
        const_ready = sem("const_ready")
        gm_ready = sem("gm_ready")
        wstep = sem("wstep")
        wt_ready = sem("wt_ready")
        wt_used = sem("wt_used")
        wmean_ready = sem("wmean_ready")
        whi_ready = sem("whi_ready")
        lw_ready = sem("lw_ready")
        h_ready = sem("h_ready")
        sq_ready = sem("sq_ready")
        sq_used = sem("sq_used")
        small_ready = sem("small_ready")
        small_used = sem("small_used")
        rstd_ready = sem("rstd_ready")
        diag_ready = sem("diag_ready")
        bc_ready = sem("bc_ready")
        rb_ready = sem("rb_ready")
        t_ready = sem("t_ready")
        act_ready = sem("act_ready")
        hi_ready = sem("hi_ready")
        split_ready = sem("split_ready")
        x1_ready = sem("x1_ready")
        ystat_ready = sem("ystat_ready")
        xstat_ready = sem("xstat_ready")
        step = sem("step")
        grstd_ready = sem("grstd_ready")
        gx_ready = sem("gx_ready")
        xse_ready = sem("xse_ready")
        out_ready = sem("out_ready")

        def at(im, per_image, k):
            return im.i * per_image + k

        setup, end = Img(-1, 1, 0, "setup"), Img(B, 0, B // 2, "end")

        def wt_row(r):
            return h[r % 2][:, 0:C // TOK, :].rearrange("p a b -> p (a b)")

        def images(eng, first, mid, last):
            first(Img(0, 0, 0, "first"))
            with eng.Fori(0, (B - 2) // 2) as j:
                mid(Img(2 * j + 1, 1, j, "mid"))
                mid(Img(2 * j + 2, 0, j + 1, "mid"))
            last(Img(B - 1, 1, (B - 2) // 2, "last"))

        def after(im):
            return Img(im.i + 1, 1 - im.slot, im.use + im.slot, "")

        def before(im):
            return Img(im.i - 1, 1 - im.slot, im.use - 1 + im.slot, "")

        block = ctx.enter_context(nc.Block())

        @block.sync
        def _(sp):
            def load_w(m, w, slot):
                sp.dma_start(x_sb[:, slot, :, 0:C], w.rearrange("(p t) c -> p t c", p=P)).then_inc(w_loaded[m], 16)

            def load_x(im):
                for half in range(2):
                    sp.dma_start(x_sb[:, im.slot, 3 * half:3 * half + 3, :],
                                 x_v[im.i, :, 3 * half:3 * half + 3, :]).then_inc(x_loaded[im.slot], 16)

            load_w(0, W1, 1)
            for n, v in enumerate((b1, b2, b3, g1, g2, beta1, beta2, Lb)):
                sp.dma_start(vec[:, n, :], v.rearrange("(p t) -> p t", p=P)).then_inc(vec_loaded, 16)
            load_w(1, W2, 0)
            sp.wait_ge(wt_ready, T)
            load_w(2, W3, 1)
            sp.wait_ge(wt_ready, 2 * T)
            load_x(Img(0, 0, 0, ""))
            sp.wait_ge(wt_ready, 3 * T)
            load_w(3, LW, 1)
            sp.wait_ge(wt_ready, 4 * T)
            load_x(Img(1, 1, 0, ""))

            def store(im):
                for half in range(2):
                    sp.wait_ge(out_ready, at(im, T, 3 * half + 3))
                    sp.dma_start(out_v[im.i, :, 3 * half:3 * half + 3, :],
                                 x_sb[:, im.slot, 3 * half:3 * half + 3, :]).then_inc(stored[im.slot], 16)

            def image(im):
                prev = before(im)
                store(prev)
                if im.kind == "mid":
                    sp.wait_ge(stored[prev.slot], (prev.use + 1) * 32)
                    load_x(after(im))

            images(sp, lambda im: None, image, image)
            last = Img(B - 1, 1, (B - 2) // 2, "")
            store(last)
            sp.wait_ge(stored[0], B // 2 * 32)
            sp.wait_ge(stored[1], B // 2 * 32)

        @block.tensor
        def _(pe):
            def use_small(n):
                if not (isinstance(n, int) and n == 0):
                    pe.wait_ge(small_used, n)

            pe.wait_ge(const_ready, 6)
            for m in range(4):
                pe.wait_ge(w_loaded[m], 16)
                slot = (m + 1) % 2 if m < 3 else 1
                for tc in range(T):
                    r = m * T + tc
                    if r - 2 >= LAYERS * T:
                        pe.wait_ge(lw_ready, r - 1 - LAYERS * T)
                    elif r >= 2:
                        pe.wait_ge(wt_used, r - 1)
                    for to in range(T):
                        mm = nc.tensor.transpose(wt_row(r)[:, to * P:(to + 1) * P], x_sb[:, slot, to, tc:C:T], ident[:])
                    mm.then_inc(wt_ready, 1)
                if m < 2:
                    use_small(m)
                    pe.wait_ge(wstep, m + 1)
                    nc.tensor.matmul(small[:, 0:1], ones[:], wmean[:, 2 * T + m:2 * T + m + 1], start=True, stop=True) \
                        .then_inc(small_ready, 1)

            def group_sum(n, src, ready, value):
                use_small(n)
                pe.wait_ge(ready, value)
                nc.tensor.matmul(small[:, 0:1], gmean[:], src, start=True, stop=True).then_inc(small_ready, 1)

            group_sum(2, gs[:, 0, 0:1], step, step_no(setup, "x_mean"))
            group_sum(3, gs[:, 0, 4:5], step, step_no(setup, "x_spread"))

            def ln_sum(im, q):
                use_small(small_no(im, f"ln{q}"))
                pe.wait_ge(sq_used, at(im, 5 * len(LN), 5 * q + 5))
                for half in range(2):
                    mm = nc.tensor.matmul(small[:, half:half + 1], sqsum[:, half * P:(half + 1) * P], ones[:, 0:1],
                                          start=True, stop=True)
                mm.then_inc(small_ready, 1)

            def ln_broadcast(im, q):
                pe.wait_ge(diag_ready, at(im, len(LN), q + 1))
                nc.tensor.matmul(bc[:, 0:TOK], ones[:], diag[:], start=True, stop=True).then_inc(bc_ready, 1)

            def squeeze(im, n):
                use_small(n)
                pe.wait_ge(xse_ready, im.i)
                for to in range(T):
                    for tc in range(T):
                        mm = nc.tensor.matmul(small[:, to:to + 1], lw[:, tc, to, :], se[:, 0, tc:tc + 1],
                                              start=(tc == 0), stop=(tc == T - 1))
                mm.then_inc(small_ready, 1)

            def extras(im, k, s):
                if k - 1 in LN:
                    if s == 0:
                        ln_sum(im, LN.index(k - 1))
                    if s == 2:
                        ln_broadcast(im, LN.index(k - 1))
                if im.kind != "first":
                    if (k, s) == (1, 0):
                        group_sum(small_no(im, "g1"), gs[:, 1, 0:1], step, step_no(im, "y_mean"))
                    if (k, s) == (1, 2):
                        group_sum(small_no(im, "g2"), gs[:, 1, 4:5], step, step_no(im, "y_spread"))
                    if (k, s) == (2, 3):
                        squeeze(im, small_no(im, "se"))
                if im.kind != "last":
                    if (k, s) == (10, 0):
                        group_sum(small_no(im, "gx1"), gs[:, 0, 0:1], step, step_no(im, "x_mean"))
                    if (k, s) == (10, 2):
                        group_sum(small_no(im, "gx2"), gs[:, 0, 4:5], step, step_no(im, "x_spread"))

            def bank_free(im, k, bank):
                planes = (bank + 1) * OPB
                if k - 2 in LN:
                    pe.wait_ge(t_ready, at(im, T * len(LN), T * LN.index(k - 2) + planes))
                elif k >= 2:
                    pe.wait_ge(x1_ready, at(im, T * TILES, T * PHASES[k - 2][1] + planes))
                elif im.kind != "first":
                    pe.wait_ge(x1_ready, at(im, T * TILES, T * (k - 2) + planes))

            def phase(im, k):
                layer, _, par = PHASES[k]
                for o in range(T):
                    if o % OPB == 0:
                        bank_free(im, k, o // OPB)
                    for c in range(T):
                        if o == 0:
                            pe.wait_ge(split_ready, at(im, NPH * T, k * T + c + 1))
                        hi, lo = a_hi[:, par, c, :], a_lo[:, par, c, :]
                        acc = h[par][:, o, :]
                        nc.tensor.matmul(acc, w_hi[:, layer, c, o, :], hi, start=(c == 0), stop=False)
                        nc.tensor.matmul(acc, w_lo[:, layer, c, o, :], hi, start=False, stop=False)
                        mm = nc.tensor.matmul(acc, w_hi[:, layer, c, o, :], lo, start=False, stop=(c == T - 1))
                    if o % OPB == OPB - 1:
                        mm.then_inc(h_ready, 1)
                    extras(im, k, o)

            def image(im):
                for k in range(NPH):
                    phase(im, k)

            pe.wait_ge(lw_ready, T)
            images(pe, image, image, image)
            group_sum(small_no(end, "g1"), gs[:, 1, 0:1], step, step_no(end, "y_mean"))
            group_sum(small_no(end, "g2"), gs[:, 1, 4:5], step, step_no(end, "y_spread"))
            squeeze(end, small_no(end, "se"))

        @block.scalar
        def _(act):
            for m in range(4):
                for tc in range(T):
                    r = m * T + tc
                    act.wait_ge(wt_ready, r + 1)
                    if m < 2:
                        act.wait_ge(wmean_ready, r + 1)
                        nc.scalar.activation(w_hi[:, m, tc, :, :].rearrange("p a b -> p (a b)"), wt_row(r),
                                             ACT.Identity, bias=wmean[:, r:r + 1], scale=1.0).then_inc(whi_ready, 1)
                    elif m == 2:
                        nc.scalar.activation(w_hi[:, m, tc, :, :].rearrange("p a b -> p (a b)"), wt_row(r),
                                             ACT.Copy).then_inc(whi_ready, 1)
                    else:
                        nc.scalar.activation(lw[:, tc, :, :].rearrange("p a b -> p (a b)"), wt_row(r),
                                             ACT.Copy).then_inc(lw_ready, 1)

            def square(im, q, o):
                k = LN[q]
                layer, _, par = PHASES[k]
                act.wait_ge(h_ready, at(im, NPH * BANKS, k * BANKS + o // OPB + 1))
                if o >= 2:
                    act.wait_ge(sq_used, at(im, 5 * len(LN), 5 * q + max(o - 2, 1)))
                elif not (im.kind == "first" and q == 0):
                    act.wait_ge(sq_used, at(im, 5 * len(LN), 5 * q - 1 + o))
                nc.scalar.activation(sq[:, o % 2, :], h[par][:, o, :], ACT.Square, bias=bias[layer][:, o:o + 1],
                                     scale=1.0).then_inc(sq_ready, 1)

            def spread(im, q):
                act.wait_ge(bc_ready, at(im, len(LN), q + 1))
                nc.scalar.activation(diag[:], bc[:, 0:TOK], ACT.Copy).then_inc(rb_ready, 1)

            def gelu(im, q, o):
                k = LN[q]
                layer = PHASES[k][0]
                act.wait_ge(t_ready, at(im, T * len(LN), T * q + o + 1))
                t = t_ring[:, o % RING, :]
                nc.scalar.activation(t, t, ACT.Gelu, bias=bet[layer][:, o:o + 1], scale=gam[layer][:, o:o + 1]) \
                    .then_inc(act_ready, 1)

            def prep(im, src, tile, k, half):
                act.wait_ge(gx_ready, src.i + 1)
                if not (isinstance(im.i, int) and im.i == 0 and k == 0 and half == 0):
                    act.wait_ge(split_ready, at(im, NPH * T, T * k + 3 * half))
                nc.scalar.activation(t_ring[:], x_sb[:, src.slot, 3 * half:3 * half + 3, tile * TOK:(tile + 1) * TOK],
                                     ACT.Identity, bias=gs[:, 0, 7:8], scale=gs[:, 0, 6:7]).then_inc(act_ready, 3)

            def phase(im, k):
                prev = LN.index(k - 1) if k - 1 in LN else None
                this = LN.index(k) if k in LN else None
                if prev is not None:
                    square(im, prev, 4)
                    square(im, prev, 5)
                if k == 0:
                    prep(im, im, 1, 1, 0)
                    prep(im, im, 1, 1, 1)
                if k in (5, 6):
                    prep(im, im, k - 3, k + 1, 0)
                    prep(im, im, k - 3, k + 1, 1)
                if k == NPH - 1 and im.kind != "last":
                    prep(im, after(im), 0, NPH, 0)
                    prep(im, after(im), 0, NPH, 1)
                if this is not None:
                    square(im, this, 0)
                    square(im, this, 1)
                if prev is not None:
                    spread(im, prev)
                    for o in range(3):
                        gelu(im, prev, o)
                if this is not None:
                    square(im, this, 2)
                    square(im, this, 3)
                if prev is not None:
                    for o in range(3, T):
                        gelu(im, prev, o)

            def image(im):
                for k in range(NPH):
                    phase(im, k)

            first = Img(0, 0, 0, "first")
            for half in range(2):
                prep(first, first, 0, 0, half)
            images(act, image, image, image)

        @block.gpsimd
        def _(pool):
            nc.gpsimd.memset(mhalf, -0.5).then_inc(const_ready, 1)
            nc.gpsimd.memset(ones[:], 1.0).then_inc(const_ready, 1)
            nc.gpsimd.memset(ident[:], 0.0).then_inc(const_ready, 1)
            nc.gpsimd.memset(gmean[:], 1.0 / PPG).then_inc(const_ready, 1)
            pool.wait_ge(const_ready, 4)
            nc.gpsimd.affine_select(out=ident[:], in_=ident[:], compare_op=ALU.not_equal, fill=1.0, base=0,
                                    pattern=[[-1, P]], channel_multiplier=1).then_inc(const_ready, 1)
            groups = gmean[:].rearrange("p (g r) -> p g r", r=PPG)
            nc.gpsimd.affine_select(out=groups, in_=groups, compare_op=ALU.is_ge, fill=0.0, base=0,
                                    pattern=[[-PPG, P // PPG], [0, PPG]], channel_multiplier=1).then_inc(gm_ready, 1)
            pool.wait_ge(gm_ready, 1)
            nc.gpsimd.affine_select(out=groups, in_=groups, compare_op=ALU.is_ge, fill=0.0, base=PPG - 1,
                                    pattern=[[PPG, P // PPG], [0, PPG]], channel_multiplier=-1).then_inc(const_ready, 1)

            def group_rstd(n, which):
                pool.wait_ge(small_used, n + 1)
                nc.gpsimd.tensor_tensor(gs[:, which, 6:7], gs[:, which, 5:6], mhalf[:, 0:1], ALU.pow) \
                    .then_inc(grstd_ready, 1)

            def add(im, q, n):
                value = at(im, T * len(LN), T * q + n + 2)
                pool.wait_ge(sq_ready, value)
                if n == 0:
                    if q > 0:
                        pool.wait_ge(small_used, small_no(im, f"ln{q - 1}") + 1)
                    elif im.kind != "first":
                        pool.wait_ge(small_used, small_no(im, "ln0") - len(NEXT))
                    nc.gpsimd.tensor_tensor(sqsum[:], sq[:, 0, :], sq[:, 1, :], ALU.add).then_inc(sq_used, 1)
                else:
                    pool.wait_ge(sq_used, at(im, 5 * len(LN), 5 * q + n))
                    nc.gpsimd.tensor_tensor(sqsum[:], sqsum[:], sq[:, (n + 1) % 2, :], ALU.add).then_inc(sq_used, 1)

            def ln_rstd(im, q):
                pool.wait_ge(small_used, small_no(im, f"ln{q}") + 1)
                nc.gpsimd.tensor_tensor(lnr, lnv, mhalf, ALU.pow).then_inc(rstd_ready, 1)

            def image(im):
                for k in range(NPH):
                    prev = LN.index(k - 1) if k - 1 in LN else None
                    this = LN.index(k) if k in LN else None
                    if prev is not None:
                        add(im, prev, 3)
                        add(im, prev, 4)
                        ln_rstd(im, prev)
                    if this is not None:
                        add(im, this, 0)
                    if k == 1 and im.kind != "first":
                        group_rstd(small_no(im, "g2"), 1)
                    if k == 10 and im.kind != "last":
                        group_rstd(small_no(im, "gx2"), 0)
                    if this is not None:
                        add(im, this, 1)
                        add(im, this, 2)

            group_rstd(3, 0)
            images(pool, image, image, image)
            group_rstd(small_no(end, "g2"), 1)

        @block.vector
        def _(dve):
            dve.wait_ge(vec_loaded, 8 * 16)
            for m in range(2):
                nc.vector.reduce_sum(wmean[:, 2 * T + m:2 * T + m + 1], bias[m], AX.X).then_inc(wstep, 1)
            for m in range(LAYERS):
                for tc in range(T):
                    r = m * T + tc
                    dve.wait_ge(wt_ready, r + 1)
                    hi = w_hi[:, m, tc, :, :].rearrange("p a b -> p (a b)").bitcast(F32)
                    lo = w_lo[:, m, tc, :, :].rearrange("p a b -> p (a b)")
                    if m < 2:
                        mean = wmean[:, r:r + 1]
                        nc.vector.reduce_sum(mean, wt_row(r), AX.X).then_inc(wstep, 1)
                        dve.wait_ge(wstep, 2 + r + 1 + 2 * m)
                        nc.vector.tensor_scalar(mean, mean, -1.0 / C, None, ALU.mult).then_inc(wmean_ready, 1)
                        dve.wait_ge(whi_ready, r + 1)
                        nc.vector.scalar_tensor_tensor(out=lo, in0=wt_row(r), scalar=mean, in1=hi,
                                                       op0=ALU.add, op1=ALU.subtract).then_inc(wt_used, 1)
                    else:
                        dve.wait_ge(whi_ready, r + 1)
                        nc.vector.tensor_tensor(lo, wt_row(r), hi, ALU.subtract).then_inc(wt_used, 1)
                if m < 2:
                    mean = wmean[:, 2 * T + 2 + m:2 * T + 3 + m]
                    dve.wait_ge(small_ready, m + 1)
                    nc.vector.tensor_scalar(mean, small[:, 0:1], -1.0 / C, None, ALU.mult).then_inc(small_used, 1)
                    dve.wait_ge(small_used, m + 1)
                    nc.vector.tensor_scalar(bias[m], bias[m], mean, None, ALU.add).then_inc(wstep, 2)

            def x_stats(im, n):
                t, piece = n // (HW // XCH), n % (HW // XCH)
                dve.wait_ge(x_loaded[im.slot], (im.use + 1) * 32)
                nc.vector.bn_stats(xstat[:, n, :], x_sb[:, im.slot, t, piece * XCH:(piece + 1) * XCH]) \
                    .then_inc(xstat_ready, 1)

            def gn_mean(im, which, name):
                if which == 0:
                    dve.wait_ge(xstat_ready, (im.i + 2) * len(XPIECES))
                    dve.nop(nofuse=True)
                    stat = xstat[:].rearrange("p a b -> p (a b)")
                else:
                    dve.wait_ge(ystat_ready, im.i * T * TILES)
                    dve.nop(nofuse=True)
                    for t in range(T):
                        nc.vector.bn_aggr(ymean[:, t, :], ystat[:, t, :, :].rearrange("p a b -> p (a b)"))
                    stat = ystat[:].rearrange("p t a b -> p (t a b)")
                nc.vector.bn_aggr(gs[:, which, 0:2], stat).then_inc(step, 1)

            def gn_spread(im, which, n, name):
                mean, var, gmean_, dev, spread_ = (gs[:, which, c:c + 1] for c in range(5))
                dve.wait_ge(small_ready, n + 1)
                nc.vector.tensor_copy(gmean_, small[:, 0:1])
                nc.vector.tensor_tensor(dev, mean, small[:, 0:1], ALU.subtract).then_inc(small_used, 1)
                dve.wait_ge(small_used, n + 1)
                nc.vector.scalar_tensor_tensor(out=spread_, in0=dev, scalar=dev, in1=var, op0=ALU.mult,
                                               op1=ALU.add).then_inc(step, 1)

            def gn_var(im, which, n):
                dve.wait_ge(small_ready, n + 1)
                nc.vector.tensor_scalar(gs[:, which, 5:6], small[:, 0:1], EPS_GN, None, ALU.add) \
                    .then_inc(small_used, 1)

            def gn_shift(count):
                dve.wait_ge(grstd_ready, count)
                nc.vector.scalar_tensor_tensor(out=gs[:, 0, 7:8], in0=gs[:, 0, 2:3], scalar=-1.0, in1=gs[:, 0, 6:7],
                                               op0=ALU.mult, op1=ALU.mult).then_inc(gx_ready, 1)

            def squeeze_input(im):
                dve.wait_ge(grstd_ready, 2 * im.i + (im.kind != "end"))
                nc.vector.tensor_scalar(se[:, 0, :], ymean[:, :, 0], gs[:, 1, 2:3], gs[:, 1, 6:7],
                                        ALU.subtract, ALU.mult).then_inc(xse_ready, 1)

            def gate(im):
                n = small_no(im, "se")
                z, gain, shift = se[:, 1, :], se[:, 2, :], se[:, 3, :]
                dve.wait_ge(small_ready, n + 1)
                nc.vector.tensor_tensor(z, small[:, 0:T], lbias, ALU.add).then_inc(small_used, 1)
                dve.wait_ge(small_used, n + 1)
                nc.vector.tensor_scalar(z, z, 1.0 / 6.0, 0.5, ALU.mult, ALU.add).then_inc(step, 1)
                dve.wait_ge(step, step_no(im, "z"))
                nc.vector.tensor_scalar(z, z, 0.0, 1.0, ALU.max, ALU.min).then_inc(step, 1)
                dve.wait_ge(step, step_no(im, "gate"))
                nc.vector.tensor_scalar(z, z, gs[:, 1, 6:7], None, ALU.mult).then_inc(step, 1)
                dve.wait_ge(step, step_no(im, "gain"))
                nc.vector.tensor_scalar(gain, z, 1.0, None, ALU.add)
                nc.vector.tensor_scalar(shift, z, gs[:, 1, 2:3], -1.0, ALU.mult, ALU.mult).then_inc(step, 1)
                dve.wait_ge(step, step_no(im, "shift"))

            def excite(im, planes):
                for o in planes:
                    plane = x_sb[:, before(im).slot, o, :]
                    nc.vector.tensor_scalar(plane, plane, se[:, 2, o:o + 1], se[:, 3, o:o + 1], ALU.mult, ALU.add) \
                        .then_inc(out_ready, 1)

            def ln_var(im, q):
                dve.wait_ge(small_ready, small_no(im, f"ln{q}") + 1)
                nc.vector.tensor_scalar(lnv, small[:, 0:2], 1.0 / C, EPS_LN, ALU.mult, ALU.add) \
                    .then_inc(small_used, 1)

            def ln_diag(im, q):
                dve.wait_ge(rstd_ready, at(im, len(LN), q + 1))
                nc.vector.tensor_tensor(diag[:].rearrange("p (a b) -> p a b", a=2),
                                        ident[:].unsqueeze(1).to_broadcast([P, 2, P]),
                                        lnr.unsqueeze(2).to_broadcast([P, 2, P]), ALU.mult).then_inc(diag_ready, 1)

            def normalise(im, q, o):
                layer, _, par = PHASES[LN[q]]
                if o == 0:
                    dve.wait_ge(rb_ready, at(im, len(LN), q + 1))
                dve.wait_ge(split_ready, at(im, NPH * T, (LN[q] + 2) * T + o - RING + 1))
                nc.vector.scalar_tensor_tensor(out=t_ring[:, o % RING, :], in0=h[par][:, o, :],
                                               scalar=bias[layer][:, o:o + 1], in1=diag[:],
                                               op0=ALU.add, op1=ALU.mult).then_inc(t_ready, 1)

            def split(im, k, o, n, between=None):
                par = PHASES[k % NPH][2]
                src = t_ring[:, o % RING:o % RING + n, :]
                hi, lo = a_hi[:, par, o:o + n, :], a_lo[:, par, o:o + n, :]
                dve.wait_ge(act_ready, at(im, NPH * T, k * T + o + n))
                nc.vector.tensor_copy(hi, src).then_inc(hi_ready, n)
                if between:
                    between()
                dve.wait_ge(hi_ready, at(im, NPH * T, k * T + o + n))
                nc.vector.tensor_tensor(lo, src, hi.bitcast(F32), ALU.subtract).then_inc(split_ready, n)

            def x1(im, tile, o):
                k = [p[:2] for p in PHASES].index((LAYERS - 1, tile))
                xs = x_sb[:, im.slot, o, tile * TOK:(tile + 1) * TOK]
                if o == 0:
                    dve.wait_ge(h_ready, at(im, NPH * BANKS, (k + 1) * BANKS))
                nc.vector.scalar_tensor_tensor(out=xs, in0=h[PHASES[k][2]][:, o, :], scalar=bias[2][:, o:o + 1], in1=xs,
                                               op0=ALU.add, op1=ALU.add).then_inc(x1_ready, 1)

            def y_stats(im, tile, o):
                dve.wait_ge(x1_ready, at(im, T * TILES, T * tile + o + 1))
                nc.vector.bn_stats(ystat[:, o, tile, :], x_sb[:, im.slot, o, tile * TOK:(tile + 1) * TOK]) \
                    .then_inc(ystat_ready, 1)

            def finish_tile(im, tile, after_planes):
                for o in range(T):
                    x1(im, tile, o)
                    if o >= 1:
                        y_stats(im, tile, o - 1)
                    for f in after_planes.get(o, ()):
                        f()
                y_stats(im, tile, T - 1)

            def phase(im, k):
                if k - 1 in LN:
                    q = LN.index(k - 1)
                    ln_var(im, q)
                    if k == 1 and im.kind != "first":
                        gn_spread(im, 1, small_no(im, "g1"), "y")
                    if k == 10 and im.kind != "last":
                        gn_spread(im, 0, small_no(im, "gx1"), "x")
                    ln_diag(im, q)
                    for o in range(RING):
                        normalise(im, q, o)
                    if k == 1 and im.kind != "first":
                        gn_var(im, 1, small_no(im, "g2"))
                    if k == 10 and im.kind != "last":
                        gn_var(im, 0, small_no(im, "gx2"))
                    for o in range(T):
                        ahead = o + RING - 1
                        split(im, k + 1, o, 1, (lambda: normalise(im, q, ahead)) if RING <= ahead < T else None)
                    if k == 1 and im.kind != "first":
                        squeeze_input(im)
                    if k == 2 and im.kind != "first":
                        gate(im)
                    if k == 3 and im.kind != "first":
                        excite(im, range(0, 3))
                    if k == 4 and im.kind != "first":
                        excite(im, range(3, T))
                    if k in (7, 8, 9) and im.kind != "last":
                        for n in range(4 * (k - 7), 4 * (k - 6)):
                            x_stats(after(im), n)
                    if k == 9 and im.kind != "last":
                        gn_mean(im, 0, "x")
                    if k == 10 and im.kind != "last":
                        gn_shift(2 * im.i + 2)
                elif k == 0 and im.kind == "first":
                    for half in range(2):
                        split(im, 1, 3 * half, 3)
                elif k == NPH - 1 and im.kind == "last":
                    finish_tile(im, 2, {})
                else:
                    src, tile = (before(im), TILES - 1) if k == 0 else (im, PHASES[k - 1][1])
                    finish_tile(src, tile, {3: [lambda: split(im, k + 1, 0, 3)], 4: [lambda: split(im, k + 1, 3, 3)]})
                    if k == 0:
                        gn_mean(im, 1, "y")

            def image(im):
                for k in range(NPH):
                    phase(im, k)

            first = Img(0, 0, 0, "first")
            for n in range(len(XPIECES)):
                x_stats(first, n)
            gn_mean(setup, 0, "x")
            gn_spread(setup, 0, 2, "x")
            gn_var(setup, 0, 3)
            gn_shift(1)
            for half in range(2):
                split(first, 0, 3 * half, 3)
            images(dve, image, image, image)
            finish_tile(Img(B - 1, 1, (B - 2) // 2, "last"), TILES - 1, {})
            gn_mean(end, 1, "y")
            gn_spread(end, 1, small_no(end, "g1"), "y")
            gn_var(end, 1, small_no(end, "g2"))
            squeeze_input(end)
            gate(end)
            excite(end, range(T))


_INS = ["x", "L0_conv_W1", "L0_conv_b1", "L0_conv_g1", "L0_conv_beta1", "L0_conv_W2", "L0_conv_b2", "L0_conv_g2",
        "L0_conv_beta2", "L0_conv_W3", "L0_conv_b3", "L1_conv_W", "L1_conv_b"]


def kernel(**inputs):
    import numpy as _np
    import concourse.bacc as _bacc
    from concourse import mybir as _mybir
    from concourse.bass_utils import run_bass_kernel_spmd as _run

    nc = _bacc.Bacc("TRN2", target_bir_lowering=False, num_devices=1)
    arrays, args = {}, []
    for name in _INS:
        a = _np.ascontiguousarray(inputs[name])
        arrays[f"in_{name}"] = a
        args.append(nc.dram_tensor(f"in_{name}", a.shape, _mybir.dt.from_np(a.dtype), kind="ExternalInput").ap())
    args.append(nc.dram_tensor("out_0", (B, C, 32, 32), _mybir.dt.float32, kind="ExternalOutput").ap())
    program(nc, *args)
    r = _run(nc, [arrays], core_ids=[0])
    return r.results[0]["out_0"]
```

```python
from contextlib import ExitStack
from typing import NamedTuple

import concourse.bass as bass
from concourse import mybir

F32 = mybir.dt.float32
F32R = mybir.dt.float32r
ALU = mybir.AluOpType
ACT = mybir.ActivationFunctionType
AX = mybir.AxisListType

P = 128
B, C, HW = 16, 768, 1024
T = C // P
CPG = C // 32
PPG = CPG // T
TOK = 256
TILES = HW // TOK
PAIRS = TILES // 2
LAYERS = 3
XCH = 512
XPIECES = range(T * HW // XCH)
RING = 3
EPS_LN = 1e-6
EPS_GN = 1e-5

PHASES = [(layer, 2 * pair + par, par) for pair in range(PAIRS) for layer in range(LAYERS) for par in range(2)]
NPH = len(PHASES)
LN = [k for k in range(NPH) if PHASES[k][0] < LAYERS - 1]
BANKS = T * TOK // 512
OPB = T // BANKS

PREV = ["g1", "g2", "se0", "se1"]
NEXT = ["gx1", "gx2"]
SMALL = ["ln0", "g1", "g2", "ln1", "se0", "ln2", "se1", "ln3", "ln4", "ln5", "ln6", "ln7", "gx1", "gx2"]
STEPS = ["y_mean", "y_spread", "z", "gate", "gain", "shift", "x_mean", "x_spread"]
PREV_STEPS = STEPS[:6]
HALVES = 2
AT_LN_SUM, AT_LN_BC, AT_G1, AT_G2, AT_SE = 8, 15, 11, 20, 11
N_SETUP_SMALL = 2 + 2


class Img(NamedTuple):
    i: object
    slot: int
    use: object
    kind: str


def small_no(im, name):
    if im.kind == "first":
        return N_SETUP_SMALL + [u for u in SMALL if u not in PREV].index(name)
    base = N_SETUP_SMALL + len(SMALL) - len(PREV) + (im.i - 1) * len(SMALL)
    if im.kind == "end":
        return base - len(NEXT) + PREV.index(name)
    return base + (SMALL if im.kind == "mid" else [u for u in SMALL if u not in NEXT]).index(name)


def step_no(im, name):
    if im.kind == "setup":
        return ["x_mean", "x_spread"].index(name) + 1
    if im.kind == "first":
        return 2 + [s for s in STEPS if s not in PREV_STEPS].index(name) + 1
    base = 2 + len(STEPS) - len(PREV_STEPS) + (im.i - 1) * len(STEPS)
    if im.kind == "end":
        base = base - (len(STEPS) - len(PREV_STEPS))
    return base + STEPS.index(name) + 1


def program(nc, x, W1, b1, g1, beta1, W2, b2, g2, beta2, W3, b3, LW, Lb, out):
    x_v = x.rearrange("b (p t) h w -> b p t (h w)", p=P)
    out_v = out.rearrange("b (p t) h w -> b p t (h w)", p=P)

    ctx = ExitStack()
    with ctx:
        def sb(name, shape, dt=F32):
            return ctx.enter_context(nc.sbuf_tensor(name, shape, dt))

        def psum(name, shape):
            return ctx.enter_context(nc.psum_tensor(name, shape, F32))

        def sem(name):
            return ctx.enter_context(nc.semaphore(name))

        h = [psum(f"h{par}", [P, T, TOK]) for par in range(2)]
        small = psum("small", [P, 512])
        bc = psum("bc", [P, 512])

        w_hi = sb("w_hi", [P, LAYERS, T, T, P], F32R)
        w_lo = sb("w_lo", [P, LAYERS, T, T, P], F32R)
        lw = sb("lw", [P, T, T, P])
        x_sb = sb("x_sb", [P, 2, T, HW])
        a_hi = sb("a_hi", [P, 2, T, TOK], F32R)
        a_lo = sb("a_lo", [P, 2, T, TOK], F32R)
        t_ring = sb("t_ring", [P, RING, TOK])
        sq = sb("sq", [P, 2, TOK])
        sqsum = sb("sqsum", [P, TOK])
        diag = sb("diag", [P, TOK])
        ident = sb("ident", [P, P])
        ones = sb("ones", [P, P])
        gmean = sb("gmean", [P, P])
        vec = sb("vec", [P, 8, T])
        bias = [vec[:, 0, :], vec[:, 1, :], vec[:, 2, :]]
        gam = [vec[:, 3, :], vec[:, 4, :]]
        bet = [vec[:, 5, :], vec[:, 6, :]]
        lbias = vec[:, 7, :]
        xstat = sb("xstat", [P, T * HW // XCH, 6])
        ystat = sb("ystat", [P, T, TILES, 6])
        scal = sb("scal", [P, 58])
        ymean = scal[:, 0:12].rearrange("p (t a) -> p t a", t=T)
        gs = scal[:, 12:28].rearrange("p (w a) -> p w a", w=2)
        lnv = scal[:, 28:30]
        lnr = scal[:, 30:32]
        mhalf = scal[:, 32:34]
        se = scal[:, 34:58].rearrange("p (w t) -> p w t", w=4)
        sacc = t_ring[:].rearrange("p a b -> p (a b)")
        wmean = ystat[:].rearrange("p t a b -> p (t a b)")[:, 0:2 * T + 4]

        w_loaded = [sem(f"w_loaded{m}") for m in range(4)]
        vec_loaded = sem("vec_loaded")
        x_loaded = [sem(f"x_loaded{s}") for s in range(2)]
        stored = [sem(f"stored{s}") for s in range(2)]
        const_ready = sem("const_ready")
        gm_ready = sem("gm_ready")
        wstep = sem("wstep")
        wt_ready = sem("wt_ready")
        wt_used = sem("wt_used")
        wmean_ready = sem("wmean_ready")
        whi_ready = sem("whi_ready")
        wsum_ready = sem("wsum_ready")
        sacc_ready = sem("sacc_ready")
        lw_ready = sem("lw_ready")
        h_ready = sem("h_ready")
        sq_ready = sem("sq_ready")
        sq_used = sem("sq_used")
        small_ready = sem("small_ready")
        small_used = sem("small_used")
        rstd_ready = sem("rstd_ready")
        diag_ready = sem("diag_ready")
        bc_ready = sem("bc_ready")
        rb_ready = sem("rb_ready")
        t_ready = sem("t_ready")
        act_ready = sem("act_ready")
        hi_ready = sem("hi_ready")
        split_ready = sem("split_ready")
        x1_ready = sem("x1_ready")
        ystat_ready = sem("ystat_ready")
        xstat_ready = sem("xstat_ready")
        step = sem("step")
        grstd_ready = sem("grstd_ready")
        gx_ready = sem("gx_ready")
        xse_ready = sem("xse_ready")
        out_ready = sem("out_ready")

        def at(im, per_image, k):
            return im.i * per_image + k

        setup, end = Img(-1, 1, 0, "setup"), Img(B, 0, B // 2, "end")

        def wt_row(r):
            return h[r % 2][:, 0:C // TOK, :].rearrange("p a b -> p (a b)")

        def images(eng, first, mid, last):
            first(Img(0, 0, 0, "first"))
            with eng.Fori(0, (B - 2) // 2) as j:
                mid(Img(2 * j + 1, 1, j, "mid"))
                mid(Img(2 * j + 2, 0, j + 1, "mid"))
            last(Img(B - 1, 1, (B - 2) // 2, "last"))

        def after(im):
            return Img(im.i + 1, 1 - im.slot, im.use + im.slot, "")

        def before(im):
            return Img(im.i - 1, 1 - im.slot, im.use - 1 + im.slot, "")

        block = ctx.enter_context(nc.Block())

        @block.sync
        def _(sp):
            def load_w(m, w, place):
                sp.dma_start(place, w.rearrange("(p t) c -> p t c", p=P)).then_inc(w_loaded[m], 16)

            def load_x(im):
                for half in range(2):
                    sp.dma_start(x_sb[:, im.slot, 3 * half:3 * half + 3, :],
                                 x_v[im.i, :, 3 * half:3 * half + 3, :]).then_inc(x_loaded[im.slot], 16)

            load_w(0, W1, x_sb[:, 1, :, 0:C])
            for n, v in enumerate((b1, b2, b3, g1, g2, beta1, beta2, Lb)):
                sp.dma_start(vec[:, n, :], v.rearrange("(p t) -> p t", p=P)).then_inc(vec_loaded, 16)
            load_x(Img(0, 0, 0, ""))
            load_w(1, W2, lw[:].rearrange("p a b c -> p a (b c)"))
            sp.wait_ge(wt_ready, T)
            load_w(2, W3, x_sb[:, 1, :, 0:C])
            sp.wait_ge(wt_ready, 3 * T)
            load_w(3, LW, x_sb[:, 1, :, 0:C])
            sp.wait_ge(wt_ready, 4 * T)
            load_x(Img(1, 1, 0, ""))

            def store(im):
                for half in range(2):
                    sp.wait_ge(out_ready, at(im, T, 3 * half + 3))
                    sp.dma_start(out_v[im.i, :, 3 * half:3 * half + 3, :],
                                 x_sb[:, im.slot, 3 * half:3 * half + 3, :]).then_inc(stored[im.slot], 16)

            def image(im):
                prev = before(im)
                store(prev)
                if im.kind == "mid":
                    sp.wait_ge(stored[prev.slot], (prev.use + 1) * 32)
                    load_x(after(im))

            images(sp, lambda im: None, image, image)
            last = Img(B - 1, 1, (B - 2) // 2, "")
            store(last)
            sp.wait_ge(stored[0], B // 2 * 32)
            sp.wait_ge(stored[1], B // 2 * 32)

        @block.tensor
        def _(pe):
            def use_small(n):
                if not (isinstance(n, int) and n == 0):
                    pe.wait_ge(small_used, n)

            def group_sum(n, src, ready, value):
                use_small(n)
                pe.wait_ge(ready, value)
                nc.tensor.matmul(small[:, 0:1], gmean[:], src, start=True, stop=True).then_inc(small_ready, 1)

            pe.wait_ge(const_ready, 6)
            for m in range(4):
                pe.wait_ge(w_loaded[m], 16)
                rows = lw[:].rearrange("p a b c -> p a (b c)") if m == 1 else x_sb[:, 1, :, 0:C]
                for tc in range(T):
                    r = m * T + tc
                    if r - 2 >= LAYERS * T:
                        pe.wait_ge(lw_ready, r - 1 - LAYERS * T)
                    elif r >= 2:
                        pe.wait_ge(wt_used, r - 1)
                    for to in range(T):
                        mm = nc.tensor.transpose(wt_row(r)[:, to * P:(to + 1) * P], rows[:, to, tc:C:T], ident[:])
                    mm.then_inc(wt_ready, 1)
                    if m == 2 and tc == T // 2 - 1:
                        group_sum(3, gs[:, 0, 4:5], step, step_no(setup, "x_spread"))
                if m < 2:
                    use_small(m)
                    pe.wait_ge(wstep, m + 1)
                    nc.tensor.matmul(small[:, 0:1], ones[:], wmean[:, 2 * T + m:2 * T + m + 1], start=True, stop=True) \
                        .then_inc(small_ready, 1)
                if m == 1:
                    group_sum(2, gs[:, 0, 0:1], step, step_no(setup, "x_mean"))

            def ln_sum(im, q):
                use_small(small_no(im, f"ln{q}"))
                pe.wait_ge(sq_used, at(im, 5 * len(LN), 5 * q + 5))
                for half in range(2):
                    mm = nc.tensor.matmul(small[:, half:half + 1], sqsum[:, half * P:(half + 1) * P], ones[:, 0:1],
                                          start=True, stop=True)
                mm.then_inc(small_ready, 1)

            def ln_broadcast(im, q):
                pe.wait_ge(diag_ready, at(im, len(LN), q + 1))
                nc.tensor.matmul(bc[:, 0:TOK], ones[:], diag[:], start=True, stop=True).then_inc(bc_ready, 1)

            def squeeze(im, n):
                use_small(small_no(im, f"se{n}"))
                pe.wait_ge(sacc_ready, at(im, HALVES * T, (n + 1 - HALVES) * T))
                for m in range(T // HALVES):
                    to = n * (T // HALVES) + m
                    mm = nc.tensor.matmul(small[:, m:m + 1], sacc[:, to * P:(to + 1) * P], ones[:, 0:1],
                                          start=True, stop=True)
                mm.then_inc(small_ready, 1)

            def extras(im, k, s):
                if k - 1 in LN and s == AT_LN_SUM:
                    ln_sum(im, LN.index(k - 1))
                if k - 1 in LN and s == AT_LN_BC:
                    ln_broadcast(im, LN.index(k - 1))
                if im.kind != "first":
                    if (k, s) == (1, AT_G1):
                        group_sum(small_no(im, "g1"), gs[:, 1, 0:1], step, step_no(im, "y_mean"))
                    if (k, s) == (1, AT_G2):
                        group_sum(small_no(im, "g2"), gs[:, 1, 4:5], step, step_no(im, "y_spread"))
                    if k in (2, 3) and s == AT_SE:
                        squeeze(im, k - 2)
                if im.kind != "last":
                    if (k, s) == (10, AT_G1):
                        group_sum(small_no(im, "gx1"), gs[:, 0, 0:1], step, step_no(im, "x_mean"))
                    if (k, s) == (10, AT_G2):
                        group_sum(small_no(im, "gx2"), gs[:, 0, 4:5], step, step_no(im, "x_spread"))

            def bank_free(im, k, bank):
                planes = (bank + 1) * OPB
                if k - 2 in LN:
                    pe.wait_ge(t_ready, at(im, T * len(LN), T * LN.index(k - 2) + planes))
                elif k >= 2:
                    pe.wait_ge(x1_ready, at(im, T * TILES, T * PHASES[k - 2][1] + planes))
                elif im.kind != "first":
                    pe.wait_ge(x1_ready, at(im, T * TILES, T * (k - 2) + planes))

            def phase(im, k):
                layer, _, par = PHASES[k]
                for o in range(T):
                    if o % OPB == 0:
                        bank_free(im, k, o // OPB)
                    for c in range(T):
                        if o == 0:
                            pe.wait_ge(split_ready, at(im, NPH * T, k * T + c + 1))
                        hi, lo = a_hi[:, par, c, :], a_lo[:, par, c, :]
                        acc = h[par][:, o, :]
                        nc.tensor.matmul(acc, w_hi[:, layer, c, o, :], hi, start=(c == 0), stop=False)
                        nc.tensor.matmul(acc, w_lo[:, layer, c, o, :], hi, start=False, stop=False)
                        mm = nc.tensor.matmul(acc, w_hi[:, layer, c, o, :], lo, start=False, stop=(c == T - 1))
                        if o % OPB == OPB - 1 and c == T - 1:
                            mm.then_inc(h_ready, 1)
                        extras(im, k, o * T + c + 1)

            def image(im):
                for k in range(NPH):
                    phase(im, k)

            pe.wait_ge(lw_ready, T)
            images(pe, image, image, image)
            group_sum(small_no(end, "g1"), gs[:, 1, 0:1], step, step_no(end, "y_mean"))
            group_sum(small_no(end, "g2"), gs[:, 1, 4:5], step, step_no(end, "y_spread"))
            for n in range(HALVES):
                squeeze(end, n)

        @block.scalar
        def _(act):
            def prep(im, src, tile, k, half):
                act.wait_ge(gx_ready, src.i + 1)
                if not (isinstance(im.i, int) and im.i == 0 and k == 0 and half == 0):
                    act.wait_ge(split_ready, at(im, NPH * T, T * k + 3 * half))
                nc.scalar.activation(t_ring[:], x_sb[:, src.slot, 3 * half:3 * half + 3, tile * TOK:(tile + 1) * TOK],
                                     ACT.Identity, bias=gs[:, 0, 7:8], scale=gs[:, 0, 6:7]).then_inc(act_ready, 3)

            def high(r):
                m, tc = r // T, r % T
                row = w_hi[:, m, tc, :, :].rearrange("p a b -> p (a b)")
                if m < 2:
                    act.wait_ge(wmean_ready, r + 1)
                    nc.scalar.activation(row, wt_row(r), ACT.Identity, bias=wmean[:, r:r + 1], scale=1.0) \
                        .then_inc(whi_ready, 1)
                else:
                    act.wait_ge(wt_ready, r + 1)
                    nc.scalar.activation(row, wt_row(r), ACT.Copy).then_inc(whi_ready, 1)

            for r in range(2 * T):
                act.wait_ge(wt_ready, r + 1)
                nc.scalar.activation(w_hi[:, r // T, r % T, :, :].rearrange("p a b -> p (a b)"), wt_row(r),
                                     ACT.Identity, accum_out=wmean[:, r:r + 1]).then_inc(wsum_ready, 1)
                if r >= 1:
                    high(r - 1)
            high(2 * T - 1)
            first = Img(0, 0, 0, "first")
            for tc in range(T):
                high(2 * T + tc)
                if tc - T // 2 + 1 in (0, 1):
                    prep(first, first, 0, 0, tc - T // 2 + 1)
            for tc in range(T):
                act.wait_ge(wt_ready, 3 * T + tc + 1)
                nc.scalar.activation(lw[:, tc, :, :].rearrange("p a b -> p (a b)"), wt_row(3 * T + tc), ACT.Copy) \
                    .then_inc(lw_ready, 1)

            def square(im, q, o):
                k = LN[q]
                layer, _, par = PHASES[k]
                act.wait_ge(h_ready, at(im, NPH * BANKS, k * BANKS + o // OPB + 1))
                if o >= 2:
                    act.wait_ge(sq_used, at(im, 5 * len(LN), 5 * q + max(o - 2, 1)))
                elif not (im.kind == "first" and q == 0):
                    act.wait_ge(sq_used, at(im, 5 * len(LN), 5 * q - 1 + o))
                nc.scalar.activation(sq[:, o % 2, :], h[par][:, o, :], ACT.Square, bias=bias[layer][:, o:o + 1],
                                     scale=1.0).then_inc(sq_ready, 1)

            def spread(im, q):
                act.wait_ge(bc_ready, at(im, len(LN), q + 1))
                nc.scalar.activation(diag[:], bc[:, 0:TOK], ACT.Copy).then_inc(rb_ready, 1)

            def gelu(im, q, o):
                k = LN[q]
                layer = PHASES[k][0]
                act.wait_ge(t_ready, at(im, T * len(LN), T * q + o + 1))
                t = t_ring[:, o % RING, :]
                nc.scalar.activation(t, t, ACT.Gelu, bias=bet[layer][:, o:o + 1], scale=gam[layer][:, o:o + 1]) \
                    .then_inc(act_ready, 1)

            def phase(im, k):
                prev = LN.index(k - 1) if k - 1 in LN else None
                this = LN.index(k) if k in LN else None
                if prev is not None:
                    square(im, prev, 4)
                    square(im, prev, 5)
                if k == 0:
                    prep(im, im, 1, 1, 0)
                    prep(im, im, 1, 1, 1)
                if k in (5, 6):
                    prep(im, im, k - 3, k + 1, 0)
                    prep(im, im, k - 3, k + 1, 1)
                if k == NPH - 1 and im.kind != "last":
                    prep(im, after(im), 0, NPH, 0)
                    prep(im, after(im), 0, NPH, 1)
                if this is not None:
                    square(im, this, 0)
                    square(im, this, 1)
                if prev is not None:
                    spread(im, prev)
                    for o in range(3):
                        gelu(im, prev, o)
                if this is not None:
                    square(im, this, 2)
                    square(im, this, 3)
                if prev is not None:
                    for o in range(3, T):
                        gelu(im, prev, o)

            def image(im):
                for k in range(NPH):
                    phase(im, k)

            images(act, image, image, image)

        @block.gpsimd
        def _(pool):
            nc.gpsimd.memset(mhalf, -0.5).then_inc(const_ready, 1)
            nc.gpsimd.memset(ones[:], 1.0).then_inc(const_ready, 1)
            nc.gpsimd.memset(ident[:], 0.0).then_inc(const_ready, 1)
            nc.gpsimd.memset(gmean[:], 1.0 / PPG).then_inc(const_ready, 1)
            pool.wait_ge(const_ready, 4)
            nc.gpsimd.affine_select(out=ident[:], in_=ident[:], compare_op=ALU.not_equal, fill=1.0, base=0,
                                    pattern=[[-1, P]], channel_multiplier=1).then_inc(const_ready, 1)
            groups = gmean[:].rearrange("p (g r) -> p g r", r=PPG)
            nc.gpsimd.affine_select(out=groups, in_=groups, compare_op=ALU.is_ge, fill=0.0, base=0,
                                    pattern=[[-PPG, P // PPG], [0, PPG]], channel_multiplier=1).then_inc(gm_ready, 1)
            pool.wait_ge(gm_ready, 1)
            nc.gpsimd.affine_select(out=groups, in_=groups, compare_op=ALU.is_ge, fill=0.0, base=PPG - 1,
                                    pattern=[[PPG, P // PPG], [0, PPG]], channel_multiplier=-1).then_inc(const_ready, 1)

            def group_rstd(n, which):
                pool.wait_ge(small_used, n + 1)
                nc.gpsimd.tensor_tensor(gs[:, which, 6:7], gs[:, which, 5:6], mhalf[:, 0:1], ALU.pow) \
                    .then_inc(grstd_ready, 1)

            def add(im, q, n):
                value = at(im, T * len(LN), T * q + n + 2)
                pool.wait_ge(sq_ready, value)
                if n == 0:
                    if q > 0:
                        pool.wait_ge(small_used, small_no(im, f"ln{q - 1}") + 1)
                    elif im.kind != "first":
                        pool.wait_ge(small_used, small_no(im, "ln0") - len(NEXT))
                    nc.gpsimd.tensor_tensor(sqsum[:], sq[:, 0, :], sq[:, 1, :], ALU.add).then_inc(sq_used, 1)
                else:
                    pool.wait_ge(sq_used, at(im, 5 * len(LN), 5 * q + n))
                    nc.gpsimd.tensor_tensor(sqsum[:], sqsum[:], sq[:, (n + 1) % 2, :], ALU.add).then_inc(sq_used, 1)

            def ln_rstd(im, q):
                pool.wait_ge(small_used, small_no(im, f"ln{q}") + 1)
                nc.gpsimd.tensor_tensor(lnr, lnv, mhalf, ALU.pow).then_inc(rstd_ready, 1)

            def image(im):
                for k in range(NPH):
                    prev = LN.index(k - 1) if k - 1 in LN else None
                    this = LN.index(k) if k in LN else None
                    if prev is not None:
                        add(im, prev, 3)
                        add(im, prev, 4)
                        ln_rstd(im, prev)
                    if this is not None:
                        add(im, this, 0)
                    if k == 1 and im.kind != "first":
                        group_rstd(small_no(im, "g2"), 1)
                    if k == 10 and im.kind != "last":
                        group_rstd(small_no(im, "gx2"), 0)
                    if this is not None:
                        add(im, this, 1)
                        add(im, this, 2)

            group_rstd(3, 0)
            images(pool, image, image, image)
            group_rstd(small_no(end, "g2"), 1)

        @block.vector
        def _(dve):
            dve.wait_ge(vec_loaded, 8 * 16)
            for m in range(2):
                nc.vector.reduce_sum(wmean[:, 2 * T + m:2 * T + m + 1], bias[m], AX.X).then_inc(wstep, 1)

            def minus_mean(r):
                dve.wait_ge(wsum_ready, r + 1)
                nc.vector.tensor_scalar(wmean[:, r:r + 1], wmean[:, r:r + 1], -1.0 / C, None, ALU.mult) \
                    .then_inc(wmean_ready, 1)

            def low(r):
                m, tc = r // T, r % T
                hi = w_hi[:, m, tc, :, :].rearrange("p a b -> p (a b)").bitcast(F32)
                lo = w_lo[:, m, tc, :, :].rearrange("p a b -> p (a b)")
                dve.wait_ge(whi_ready, r + 1)
                if m < 2:
                    nc.vector.scalar_tensor_tensor(out=lo, in0=wt_row(r), scalar=wmean[:, r:r + 1], in1=hi,
                                                   op0=ALU.add, op1=ALU.subtract).then_inc(wt_used, 1)
                else:
                    nc.vector.tensor_tensor(lo, wt_row(r), hi, ALU.subtract).then_inc(wt_used, 1)

            def centre_bias(m):
                mean = wmean[:, 2 * T + 2 + m:2 * T + 3 + m]
                dve.wait_ge(small_ready, m + 1)
                nc.vector.tensor_scalar(mean, small[:, 0:1], -1.0 / C, None, ALU.mult).then_inc(small_used, 1)
                dve.wait_ge(small_used, m + 1)
                nc.vector.tensor_scalar(bias[m], bias[m], mean, None, ALU.add).then_inc(wstep, 1)

            def x_stats(im, n):
                t, piece = n // (HW // XCH), n % (HW // XCH)
                dve.wait_ge(x_loaded[im.slot], (im.use + 1) * 32)
                nc.vector.bn_stats(xstat[:, n, :], x_sb[:, im.slot, t, piece * XCH:(piece + 1) * XCH]) \
                    .then_inc(xstat_ready, 1)

            def gn_mean(im, which, name):
                if which == 0:
                    dve.wait_ge(xstat_ready, (im.i + 2) * len(XPIECES))
                    dve.nop(nofuse=True)
                    stat = xstat[:].rearrange("p a b -> p (a b)")
                else:
                    dve.wait_ge(ystat_ready, im.i * T * TILES)
                    dve.nop(nofuse=True)
                    for t in range(T):
                        nc.vector.bn_aggr(ymean[:, t, :], ystat[:, t, :, :].rearrange("p a b -> p (a b)"))
                    stat = ystat[:].rearrange("p t a b -> p (t a b)")
                nc.vector.bn_aggr(gs[:, which, 0:2], stat).then_inc(step, 1)

            def gn_spread(im, which, n, name):
                mean, var, gmean_, dev, spread_ = (gs[:, which, c:c + 1] for c in range(5))
                dve.wait_ge(small_ready, n + 1)
                nc.vector.tensor_copy(gmean_, small[:, 0:1])
                nc.vector.tensor_tensor(dev, mean, small[:, 0:1], ALU.subtract).then_inc(small_used, 1)
                dve.wait_ge(small_used, n + 1)
                nc.vector.scalar_tensor_tensor(out=spread_, in0=dev, scalar=dev, in1=var, op0=ALU.mult,
                                               op1=ALU.add).then_inc(step, 1)

            def gn_var(im, which, n):
                dve.wait_ge(small_ready, n + 1)
                nc.vector.tensor_scalar(gs[:, which, 5:6], small[:, 0:1], EPS_GN, None, ALU.add) \
                    .then_inc(small_used, 1)

            def gn_shift(count):
                dve.wait_ge(grstd_ready, count)
                nc.vector.scalar_tensor_tensor(out=gs[:, 0, 7:8], in0=gs[:, 0, 2:3], scalar=-1.0, in1=gs[:, 0, 6:7],
                                               op0=ALU.mult, op1=ALU.mult).then_inc(gx_ready, 1)

            def squeeze_input(im):
                dve.wait_ge(grstd_ready, 2 * im.i + (im.kind != "end"))
                nc.vector.tensor_scalar(se[:, 0, :], ymean[:, :, 0], gs[:, 1, 2:3], gs[:, 1, 6:7],
                                        ALU.subtract, ALU.mult).then_inc(xse_ready, 1)

            def squeeze(im, n):
                cols = slice(n * C // HALVES, (n + 1) * C // HALVES)
                count = at(im, HALVES * T, (n - HALVES) * T)
                for tc in range(T):
                    w = lw[:, tc, :, :].rearrange("p a b -> p (a b)")[:, cols]
                    if tc == 0:
                        dve.wait_ge(xse_ready, im.i)
                        last = im.i * NPH * T if im.kind == "end" else at(im, NPH * T, (3 + n) * T)
                        dve.wait_ge(split_ready, last)
                        nc.vector.tensor_scalar(sacc[:, cols], w, se[:, 0, tc:tc + 1], None, ALU.mult) \
                            .then_inc(sacc_ready, 1)
                    else:
                        dve.wait_ge(sacc_ready, count + tc)
                        nc.vector.scalar_tensor_tensor(out=sacc[:, cols], in0=w, scalar=se[:, 0, tc:tc + 1],
                                                       in1=sacc[:, cols], op0=ALU.mult, op1=ALU.add) \
                            .then_inc(sacc_ready, 1)

            def squeeze_bias(im, n):
                no, half = small_no(im, f"se{n}"), slice(n * T // HALVES, (n + 1) * T // HALVES)
                dve.wait_ge(small_ready, no + 1)
                nc.vector.tensor_tensor(se[:, 1, half], small[:, 0:T // HALVES], lbias[:, half], ALU.add) \
                    .then_inc(small_used, 1)

            def gate(im):
                z, gain, shift = se[:, 1, :], se[:, 2, :], se[:, 3, :]
                dve.wait_ge(small_used, small_no(im, f"se{HALVES - 1}") + 1)
                nc.vector.tensor_scalar(z, z, 1.0 / 6.0, 0.5, ALU.mult, ALU.add).then_inc(step, 1)
                dve.wait_ge(step, step_no(im, "z"))
                nc.vector.tensor_scalar(z, z, 0.0, 1.0, ALU.max, ALU.min).then_inc(step, 1)
                dve.wait_ge(step, step_no(im, "gate"))
                nc.vector.tensor_scalar(z, z, gs[:, 1, 6:7], None, ALU.mult).then_inc(step, 1)
                dve.wait_ge(step, step_no(im, "gain"))
                nc.vector.tensor_scalar(gain, z, 1.0, None, ALU.add)
                nc.vector.tensor_scalar(shift, z, gs[:, 1, 2:3], -1.0, ALU.mult, ALU.mult).then_inc(step, 1)
                dve.wait_ge(step, step_no(im, "shift"))

            def excite(im, planes):
                for o in planes:
                    plane = x_sb[:, before(im).slot, o, :]
                    nc.vector.tensor_scalar(plane, plane, se[:, 2, o:o + 1], se[:, 3, o:o + 1], ALU.mult, ALU.add) \
                        .then_inc(out_ready, 1)

            def ln_var(im, q):
                dve.wait_ge(small_ready, small_no(im, f"ln{q}") + 1)
                nc.vector.tensor_scalar(lnv, small[:, 0:2], 1.0 / C, EPS_LN, ALU.mult, ALU.add) \
                    .then_inc(small_used, 1)

            def ln_diag(im, q):
                dve.wait_ge(rstd_ready, at(im, len(LN), q + 1))
                nc.vector.tensor_tensor(diag[:].rearrange("p (a b) -> p a b", a=2),
                                        ident[:].unsqueeze(1).to_broadcast([P, 2, P]),
                                        lnr.unsqueeze(2).to_broadcast([P, 2, P]), ALU.mult).then_inc(diag_ready, 1)

            def normalise(im, q, o):
                layer, _, par = PHASES[LN[q]]
                if o == 0:
                    dve.wait_ge(rb_ready, at(im, len(LN), q + 1))
                dve.wait_ge(split_ready, at(im, NPH * T, (LN[q] + 2) * T + o - RING + 1))
                nc.vector.scalar_tensor_tensor(out=t_ring[:, o % RING, :], in0=h[par][:, o, :],
                                               scalar=bias[layer][:, o:o + 1], in1=diag[:],
                                               op0=ALU.add, op1=ALU.mult).then_inc(t_ready, 1)

            def split(im, k, o, n, between=None):
                par = PHASES[k % NPH][2]
                src = t_ring[:, o % RING:o % RING + n, :]
                hi, lo = a_hi[:, par, o:o + n, :], a_lo[:, par, o:o + n, :]
                dve.wait_ge(act_ready, at(im, NPH * T, k * T + o + n))
                nc.vector.tensor_copy(hi, src).then_inc(hi_ready, n)
                if between:
                    between()
                dve.wait_ge(hi_ready, at(im, NPH * T, k * T + o + n))
                nc.vector.tensor_tensor(lo, src, hi.bitcast(F32), ALU.subtract).then_inc(split_ready, n)

            def x1(im, tile, o):
                k = [p[:2] for p in PHASES].index((LAYERS - 1, tile))
                xs = x_sb[:, im.slot, o, tile * TOK:(tile + 1) * TOK]
                if o == 0:
                    dve.wait_ge(h_ready, at(im, NPH * BANKS, (k + 1) * BANKS))
                nc.vector.scalar_tensor_tensor(out=xs, in0=h[PHASES[k][2]][:, o, :], scalar=bias[2][:, o:o + 1], in1=xs,
                                               op0=ALU.add, op1=ALU.add).then_inc(x1_ready, 1)

            def y_stats(im, tile, o):
                dve.wait_ge(x1_ready, at(im, T * TILES, T * tile + o + 1))
                nc.vector.bn_stats(ystat[:, o, tile, :], x_sb[:, im.slot, o, tile * TOK:(tile + 1) * TOK]) \
                    .then_inc(ystat_ready, 1)

            def finish_tile(im, tile, after_planes):
                for o in range(T):
                    x1(im, tile, o)
                    if o >= 1:
                        y_stats(im, tile, o - 1)
                    for f in after_planes.get(o, ()):
                        f()
                y_stats(im, tile, T - 1)

            def phase(im, k):
                prev, nxt = im.kind != "first", im.kind != "last"
                if k - 1 in LN:
                    q = LN.index(k - 1)
                    if k in (2, 3) and prev:
                        squeeze(im, k - 2)
                    if k in (8, 9) and nxt:
                        for n in range(6 * (k - 8), 6 * (k - 8) + 4):
                            x_stats(after(im), n)
                    ln_var(im, q)
                    if k == 1 and prev:
                        gn_spread(im, 1, small_no(im, "g1"), "y")
                    if k == 10 and nxt:
                        gn_spread(im, 0, small_no(im, "gx1"), "x")
                    ln_diag(im, q)
                    if k in (2, 3) and prev:
                        squeeze_bias(im, k - 2)
                    for o in range(RING):
                        normalise(im, q, o)
                    for o in range(T):
                        ahead = o + RING - 1
                        split(im, k + 1, o, 1, (lambda: normalise(im, q, ahead)) if RING <= ahead < T else None)
                        if o == 1 and k == 1 and prev:
                            gn_var(im, 1, small_no(im, "g2"))
                        if o == 1 and k == 10 and nxt:
                            gn_var(im, 0, small_no(im, "gx2"))
                    if k == 1 and prev:
                        squeeze_input(im)
                    if k == 3 and prev:
                        gate(im)
                    if k == 4 and prev:
                        excite(im, range(0, T // 2))
                    if k in (8, 9) and nxt:
                        for n in range(6 * (k - 8) + 4, 6 * (k - 8) + 6):
                            x_stats(after(im), n)
                    if k == 9 and nxt:
                        gn_mean(im, 0, "x")
                    if k == 10 and nxt:
                        gn_shift(2 * im.i + 2)
                elif k == 0 and im.kind == "first":
                    for half in range(2):
                        split(im, 1, 3 * half, 3)
                elif k == NPH - 1 and im.kind == "last":
                    finish_tile(im, 2, {})
                else:
                    src, tile = (before(im), TILES - 1) if k == 0 else (im, PHASES[k - 1][1])
                    finish_tile(src, tile, {3: [lambda: split(im, k + 1, 0, 3)], 4: [lambda: split(im, k + 1, 3, 3)]})
                    if k == 0:
                        gn_mean(im, 1, "y")
                    if k == 5 and prev:
                        excite(im, range(T // 2, T))

            def image(im):
                for k in range(NPH):
                    phase(im, k)

            def low_and_next_mean(r):
                if r + 1 < 2 * T:
                    minus_mean(r + 1)
                low(r)

            first = Img(0, 0, 0, "first")
            minus_mean(0)
            for r in range(T):
                low_and_next_mean(r)
            centre_bias(0)
            for n in range(len(XPIECES)):
                x_stats(first, n)
            gn_mean(setup, 0, "x")
            for r in range(T, 2 * T):
                low_and_next_mean(r)
            centre_bias(1)
            gn_spread(setup, 0, 2, "x")
            for tc in range(T):
                low(2 * T + tc)
                if tc == T // 2 - 1:
                    gn_var(setup, 0, 3)
                    gn_shift(1)
                if tc - T // 2 + 1 in (0, 1):
                    split(first, 0, 3 * (tc - T // 2 + 1), 3)
            images(dve, image, image, image)
            finish_tile(Img(B - 1, 1, (B - 2) // 2, "last"), TILES - 1, {})
            gn_mean(end, 1, "y")
            gn_spread(end, 1, small_no(end, "g1"), "y")
            gn_var(end, 1, small_no(end, "g2"))
            squeeze_input(end)
            for n in range(HALVES):
                squeeze(end, n)
                squeeze_bias(end, n)
            gate(end)
            excite(end, range(T))


_INS = ["x", "L0_conv_W1", "L0_conv_b1", "L0_conv_g1", "L0_conv_beta1", "L0_conv_W2", "L0_conv_b2", "L0_conv_g2",
        "L0_conv_beta2", "L0_conv_W3", "L0_conv_b3", "L1_conv_W", "L1_conv_b"]


def kernel(**inputs):
    import numpy as _np
    import concourse.bacc as _bacc
    from concourse import mybir as _mybir
    from concourse.bass_utils import run_bass_kernel_spmd as _run

    nc = _bacc.Bacc("TRN2", target_bir_lowering=False, num_devices=1)
    arrays, args = {}, []
    for name in _INS:
        a = _np.ascontiguousarray(inputs[name])
        arrays[f"in_{name}"] = a
        args.append(nc.dram_tensor(f"in_{name}", a.shape, _mybir.dt.from_np(a.dtype), kind="ExternalInput").ap())
    args.append(nc.dram_tensor("out_0", (B, C, 32, 32), _mybir.dt.float32, kind="ExternalOutput").ap())
    program(nc, *args)
    r = _run(nc, [arrays], core_ids=[0])
    return r.results[0]["out_0"]
```

```python
from contextlib import ExitStack
from typing import NamedTuple

import concourse.bass as bass
from concourse import mybir

F32 = mybir.dt.float32
F32R = mybir.dt.float32r
ALU = mybir.AluOpType
ACT = mybir.ActivationFunctionType
AX = mybir.AxisListType

P = 128
B, C, HW = 16, 768, 1024
T = C // P
CPG = C // 32
PPG = CPG // T
TOK = 256
TILES = HW // TOK
PAIRS = TILES // 2
LAYERS = 3
XCH = 512
XPIECES = range(T * HW // XCH)
X_STATS = {8: (range(0, 4), range(4, 5), range(5, 7)), 9: (range(7, 8), range(8, 9), range(9, 12))}
RING = 3
EPS_LN = 1e-6
EPS_GN = 1e-5

PHASES = [(layer, 2 * pair + par, par) for pair in range(PAIRS) for layer in range(LAYERS) for par in range(2)]
NPH = len(PHASES)
LN = [k for k in range(NPH) if PHASES[k][0] < LAYERS - 1]
BANKS = T * TOK // 512
OPB = T // BANKS

PREV = ["g1", "g2", "se0", "se1"]
NEXT = ["gx1", "gx2"]
SMALL = ["ln0", "g1", "g2", "ln1", "se0", "ln2", "se1", "ln3", "ln4", "ln5", "ln6", "ln7", "gx1", "gx2"]
STEPS = ["y_mean", "y_spread", "z", "gate", "gain", "shift", "x_mean", "x_spread"]
PREV_STEPS = STEPS[:6]
HALVES = 2
END_PLANES = range(0, 4)
PAIR_COLS = 2 * P
LW_PAIRS = T * C // PAIR_COLS
AT_LW = [19, 27, 30, 33]
FIRST_STATS = T + 1
W_ROWS = 3
AT_LN_SUM, AT_LN_BC, AT_G1, AT_G2, AT_SE = 8, (15, 18), 10, 20, 14
N_SETUP_SMALL = 2 + 2


class Img(NamedTuple):
    i: object
    slot: int
    use: object
    kind: str


def small_no(im, name):
    if im.kind == "first":
        return N_SETUP_SMALL + [u for u in SMALL if u not in PREV].index(name)
    base = N_SETUP_SMALL + len(SMALL) - len(PREV) + (im.i - 1) * len(SMALL)
    if im.kind == "end":
        return base - len(NEXT) + PREV.index(name)
    return base + (SMALL if im.kind == "mid" else [u for u in SMALL if u not in NEXT]).index(name)


def step_no(im, name):
    if im.kind == "setup":
        return ["x_mean", "x_spread"].index(name) + 1
    if im.kind == "first":
        return 2 + [s for s in STEPS if s not in PREV_STEPS].index(name) + 1
    base = 2 + len(STEPS) - len(PREV_STEPS) + (im.i - 1) * len(STEPS)
    if im.kind == "end":
        base = base - (len(STEPS) - len(PREV_STEPS))
    return base + STEPS.index(name) + 1


def program(nc, x, W1, b1, g1, beta1, W2, b2, g2, beta2, W3, b3, LW, Lb, out):
    x_v = x.rearrange("b (p t) h w -> b p t (h w)", p=P)
    out_v = out.rearrange("b (p t) h w -> b p t (h w)", p=P)

    ctx = ExitStack()
    with ctx:
        def sb(name, shape, dt=F32):
            return ctx.enter_context(nc.sbuf_tensor(name, shape, dt))

        def psum(name, shape):
            return ctx.enter_context(nc.psum_tensor(name, shape, F32))

        def sem(name):
            return ctx.enter_context(nc.semaphore(name))

        products = psum("products", [P, 2, T, TOK])
        h = [products[:, par] for par in range(2)]
        small = psum("small", [P, 512])
        bc = psum("bc", [P, 512])

        w_hi = sb("w_hi", [P, LAYERS, T, T, P], F32R)
        w_lo = sb("w_lo", [P, LAYERS, T, T, P], F32R)
        lw = sb("lw", [P, T, T, P])
        x_sb = sb("x_sb", [P, 2, T, HW])
        a_hi = sb("a_hi", [P, 2, T, TOK], F32R)
        a_lo = sb("a_lo", [P, 2, T, TOK], F32R)
        t_ring = sb("t_ring", [P, RING, TOK])
        sqsum = sb("sqsum", [P, TOK])
        sq = sb("sq", [P, TOK])
        rstd_all = sb("rstd_all", [P, TOK])
        diag = sb("diag", [P, TOK], F32R)
        ident = sb("ident", [P, P])
        ones_r = sb("ones", [P, P], F32R)
        ones = ones_r[:].bitcast(F32)
        gmean = sb("gmean", [P, P])
        vec = sb("vec", [P, 8, T])
        bias = [vec[:, 0, :], vec[:, 1, :], vec[:, 2, :]]
        gam = [vec[:, 3, :], vec[:, 4, :]]
        bet = [vec[:, 5, :], vec[:, 6, :]]
        lbias = vec[:, 7, :]
        xstat = sb("xstat", [P, T * HW // XCH, 6])
        ystat = sb("ystat", [P, T, TILES, 6])
        scal = sb("scal", [P, 58])
        ymean = scal[:, 0:12].rearrange("p (t a) -> p t a", t=T)
        gs = scal[:, 12:28].rearrange("p (w a) -> p w a", w=2)
        lnv = scal[:, 28:30]
        lnr = scal[:, 30:32]
        lnr_hi = sb("lnr_hi", [P, 2], F32R)
        lnr_lo = sb("lnr_lo", [P, 2], F32R)
        mhalf = scal[:, 32:34]
        se = scal[:, 34:58].rearrange("p (w t) -> p w t", w=4)
        sacc = t_ring[:].rearrange("p a b -> p (a b)")
        wmean = ystat[:].rearrange("p t a b -> p (t a b)")[:, 0:2 * T + 4]

        w_loaded = [sem(f"w_loaded{m}") for m in range(4)]
        vec_loaded = sem("vec_loaded")
        x_loaded = [sem(f"x_loaded{s}") for s in range(2)]
        stored = [sem(f"stored{s}") for s in range(2)]
        const_ready = sem("const_ready")
        gm_ready = sem("gm_ready")
        wstep = sem("wstep")
        wt_ready = sem("wt_ready")
        wt_used = sem("wt_used")
        wmean_ready = sem("wmean_ready")
        whi_ready = sem("whi_ready")
        wsum_ready = sem("wsum_ready")
        sacc_ready = sem("sacc_ready")
        lwt_ready = sem("lwt_ready")
        lw_ready = sem("lw_ready")
        h_ready = sem("h_ready")
        sq_ready = sem("sq_ready")
        sq_used = sem("sq_used")
        small_ready = sem("small_ready")
        small_used = sem("small_used")
        rstd_ready = sem("rstd_ready")
        rhi_ready = sem("rhi_ready")
        rlo_ready = sem("rlo_ready")
        diag_ready = sem("diag_ready")
        diag_used = sem("diag_used")
        bc_ready = sem("bc_ready")
        rb_ready = sem("rb_ready")
        t_ready = sem("t_ready")
        act_ready = sem("act_ready")
        hi_ready = sem("hi_ready")
        split_ready = sem("split_ready")
        x1_ready = sem("x1_ready")
        ystat_ready = sem("ystat_ready")
        xstat_ready = sem("xstat_ready")
        step = sem("step")
        grstd_ready = sem("grstd_ready")
        gx_ready = sem("gx_ready")
        xse_ready = sem("xse_ready")
        out_ready = sem("out_ready")

        def at(im, per_image, k):
            return im.i * per_image + k

        setup, end = Img(-1, 1, 0, "setup"), Img(B, 0, B // 2, "end")

        def pairs_before(k):
            return min(max(k - 1, 0) * len(AT_LW), LW_PAIRS)

        def wt_row(r):
            start = r % W_ROWS * 1024
            return products[:].rearrange("p a b c -> p (a b c)")[:, start:start + C]

        def squeeze_planes(im, n):
            return END_PLANES if im.kind == "end" else range(n * T // HALVES, (n + 1) * T // HALVES)

        def images(eng, first, mid, last):
            first(Img(0, 0, 0, "first"))
            with eng.Fori(0, (B - 2) // 2) as j:
                mid(Img(2 * j + 1, 1, j, "mid"))
                mid(Img(2 * j + 2, 0, j + 1, "mid"))
            last(Img(B - 1, 1, (B - 2) // 2, "last"))

        def after(im):
            return Img(im.i + 1, 1 - im.slot, im.use + im.slot, "")

        def before(im):
            return Img(im.i - 1, 1 - im.slot, im.use - 1 + im.slot, "")

        block = ctx.enter_context(nc.Block())

        @block.sync
        def _(sp):
            def load_w(m, w, place):
                sp.dma_start(place, w.rearrange("(p t) c -> p t c", p=P)).then_inc(w_loaded[m], 16)

            def load_x(im):
                for half in range(2):
                    sp.dma_start(x_sb[:, im.slot, 3 * half:3 * half + 3, :],
                                 x_v[im.i, :, 3 * half:3 * half + 3, :]).then_inc(x_loaded[im.slot], 16)

            load_w(0, W1, x_sb[:, 1, :, 0:C])
            for n, v in enumerate((b1, b2, b3, g1, g2, beta1, beta2, Lb)):
                sp.dma_start(vec[:, n, :], v.rearrange("(p t) -> p t", p=P)).then_inc(vec_loaded, 16)
            load_w(1, W2, lw[:].rearrange("p a b c -> p a (b c)"))
            load_x(Img(0, 0, 0, ""))
            sp.wait_ge(wt_ready, T)
            load_w(2, W3, x_sb[:, 1, :, 0:C])
            sp.wait_ge(wt_ready, 3 * T)
            load_w(3, LW, x_sb[:, 1, :, 0:C])
            sp.wait_ge(lwt_ready, LW_PAIRS)
            load_x(Img(1, 1, 0, ""))

            def store(im, pieces):
                n = T // pieces
                for t in range(0, T, n):
                    sp.wait_ge(out_ready, at(im, T, t + n))
                    sp.dma_start(out_v[im.i, :, t:t + n, :], x_sb[:, im.slot, t:t + n, :]) \
                        .then_inc(stored[im.slot], 16)

            def image(im):
                prev = before(im)
                store(prev, 2)
                if im.kind == "mid":
                    sp.wait_ge(stored[prev.slot], (prev.use + 1) * 32)
                    load_x(after(im))

            images(sp, lambda im: None, image, image)
            last = Img(B - 1, 1, (B - 2) // 2, "")
            store(last, T)
            sp.wait_ge(stored[0], B // 2 * 32)
            sp.wait_ge(stored[1], (B // 2 - 1) * 32 + T * 16)

        @block.tensor
        def _(pe):
            def use_small(n):
                if not (isinstance(n, int) and n == 0):
                    pe.wait_ge(small_used, n)

            def group_sum(n, src, ready, value):
                use_small(n)
                pe.wait_ge(ready, value)
                nc.tensor.matmul(small[:, 0:1], gmean[:], src, start=True, stop=True).then_inc(small_ready, 1)

            pe.wait_ge(const_ready, 7)
            for m in range(LAYERS):
                pe.wait_ge(w_loaded[m], 16)
                rows = lw[:].rearrange("p a b c -> p a (b c)") if m == 1 else x_sb[:, 1, :, 0:C]
                for tc in range(T):
                    r = m * T + tc
                    if r >= W_ROWS:
                        pe.wait_ge(wt_used, r - W_ROWS + 1)
                    for to in range(T):
                        mm = nc.tensor.transpose(wt_row(r)[:, to * P:(to + 1) * P], rows[:, to, tc:C:T], ident[:])
                    mm.then_inc(wt_ready, 1)
                    if m == 2 and tc == T - 3:
                        group_sum(2, gs[:, 0, 0:1], step, step_no(setup, "x_mean"))
                    if m == 2 and tc == T - 2:
                        group_sum(3, gs[:, 0, 4:5], step, step_no(setup, "x_spread"))
                if m < 2:
                    use_small(m)
                    pe.wait_ge(wstep, m + 1)
                    nc.tensor.matmul(small[:, 0:1], ones, wmean[:, 2 * T + m:2 * T + m + 1], start=True, stop=True) \
                        .then_inc(small_ready, 1)

            def ln_sum(im, q):
                use_small(small_no(im, f"ln{q}"))
                pe.wait_ge(sq_used, at(im, 5 * len(LN), 5 * q + 5))
                for half in range(2):
                    mm = nc.tensor.matmul(small[:, half:half + 1], sqsum[:, half * P:(half + 1) * P], ones[:, 0:1],
                                          start=True, stop=True)
                mm.then_inc(small_ready, 1)

            def ln_broadcast(im, q, part):
                if im.kind == "first" and part == 0:
                    pe.wait_ge(lw_ready, pairs_before(LN[q] + 1))
                pe.wait_ge(diag_ready, at(im, 2 * len(LN), 2 * q + part + 1))
                nc.tensor.matmul(bc[:, 0:TOK], ones_r[:], diag[:], start=(part == 0), stop=(part == 1)) \
                    .then_inc(bc_ready if part else diag_used, 1)

            def squeeze(im, n):
                use_small(small_no(im, f"se{n}"))
                pe.wait_ge(sacc_ready, at(im, HALVES * T, (n + 1 - HALVES) * T))
                for m, to in enumerate(squeeze_planes(im, n)):
                    mm = nc.tensor.matmul(small[:, m:m + 1], sacc[:, to * P:(to + 1) * P], ones[:, 0:1],
                                          start=True, stop=True)
                mm.then_inc(small_ready, 1)

            def lw_transpose(n):
                tc, to = n // (T // 2), 2 * (n % (T // 2))
                pe.wait_ge(w_loaded[3], 16)
                pe.wait_ge(lw_ready, n)
                for b in range(2):
                    mm = nc.tensor.transpose(bc[:, TOK + b * P:TOK + (b + 1) * P],
                                             x_sb[:, 1, to + b, tc:C:T], ident[:])
                mm.then_inc(lwt_ready, 1)

            def extras(im, k, s):
                if k - 1 in LN and s == AT_LN_SUM:
                    ln_sum(im, LN.index(k - 1))
                if k - 1 in LN and s in AT_LN_BC:
                    ln_broadcast(im, LN.index(k - 1), AT_LN_BC.index(s))
                if im.kind == "first" and s in AT_LW:
                    n = pairs_before(k) + AT_LW.index(s)
                    if n < pairs_before(k + 1):
                        if k - 1 in LN:
                            pe.wait_ge(rb_ready, LN.index(k - 1) + 1)
                        lw_transpose(n)
                if im.kind != "first":
                    if (k, s) == (1, AT_G1):
                        group_sum(small_no(im, "g1"), gs[:, 1, 0:1], step, step_no(im, "y_mean"))
                    if (k, s) == (1, AT_G2):
                        group_sum(small_no(im, "g2"), gs[:, 1, 4:5], step, step_no(im, "y_spread"))
                    if k in (2, 3) and s == AT_SE:
                        squeeze(im, k - 2)
                if im.kind != "last":
                    if (k, s) == (10, AT_G1):
                        group_sum(small_no(im, "gx1"), gs[:, 0, 0:1], step, step_no(im, "x_mean"))
                    if (k, s) == (10, AT_G2):
                        group_sum(small_no(im, "gx2"), gs[:, 0, 4:5], step, step_no(im, "x_spread"))

            def bank_free(im, k, bank):
                planes = (bank + 1) * OPB
                if k - 2 in LN:
                    pe.wait_ge(t_ready, at(im, T * len(LN), T * LN.index(k - 2) + planes))
                elif k >= 2:
                    pe.wait_ge(x1_ready, at(im, T * TILES, T * PHASES[k - 2][1] + planes))
                elif im.kind != "first":
                    pe.wait_ge(x1_ready, at(im, T * TILES, T * (k - 2) + planes))

            def phase(im, k):
                layer, _, par = PHASES[k]
                for o in range(T):
                    if o % OPB == 0:
                        bank_free(im, k, o // OPB)
                    for c in range(T):
                        if o == 0:
                            pe.wait_ge(split_ready, at(im, NPH * T, k * T + c + 1))
                        hi, lo = a_hi[:, par, c, :], a_lo[:, par, c, :]
                        acc = h[par][:, o, :]
                        nc.tensor.matmul(acc, w_hi[:, layer, c, o, :], hi, start=(c == 0), stop=False)
                        nc.tensor.matmul(acc, w_lo[:, layer, c, o, :], hi, start=False, stop=False)
                        mm = nc.tensor.matmul(acc, w_hi[:, layer, c, o, :], lo, start=False, stop=(c == T - 1))
                        if o % OPB == OPB - 1 and c == T - 1:
                            mm.then_inc(h_ready, 1)
                        extras(im, k, o * T + c + 1)

            def image(im):
                for k in range(NPH):
                    phase(im, k)

            pe.wait_ge(wt_used, LAYERS * T)
            images(pe, image, image, image)
            group_sum(small_no(end, "g1"), gs[:, 1, 0:1], step, step_no(end, "y_mean"))
            group_sum(small_no(end, "g2"), gs[:, 1, 4:5], step, step_no(end, "y_spread"))
            use_small(small_no(end, "se0"))
            pe.wait_ge(xse_ready, B)
            for to in range(END_PLANES.stop, T):
                for tc in range(T):
                    nc.tensor.matmul(small[:, to:to + 1], lw[:, tc, to, :], se[:, 0, tc:tc + 1],
                                     start=(tc == 0), stop=(tc == T - 1))
            squeeze(end, 0)

        @block.scalar
        def _(act):
            def prep(im, src, tile, k, half):
                act.wait_ge(gx_ready, src.i + 1)
                if not (isinstance(im.i, int) and im.i == 0 and k == 0 and half == 0):
                    act.wait_ge(split_ready, at(im, NPH * T, T * k + 3 * half))
                nc.scalar.activation(t_ring[:], x_sb[:, src.slot, 3 * half:3 * half + 3, tile * TOK:(tile + 1) * TOK],
                                     ACT.Identity, bias=gs[:, 0, 7:8], scale=gs[:, 0, 6:7]).then_inc(act_ready, 3)

            def high(r):
                m, tc = r // T, r % T
                row = w_hi[:, m, tc, :, :].rearrange("p a b -> p (a b)")
                if m < 2:
                    act.wait_ge(wmean_ready, r + 1)
                    nc.scalar.activation(row, wt_row(r), ACT.Identity, bias=wmean[:, r:r + 1], scale=1.0) \
                        .then_inc(whi_ready, 1)
                else:
                    act.wait_ge(wt_ready, r + 1)
                    nc.scalar.activation(row, wt_row(r), ACT.Copy).then_inc(whi_ready, 1)

            for r in range(2 * T):
                act.wait_ge(wt_ready, r + 1)
                nc.scalar.activation(w_hi[:, r // T, r % T, :, :].rearrange("p a b -> p (a b)"), wt_row(r),
                                     ACT.Identity, accum_out=wmean[:, r:r + 1]).then_inc(wsum_ready, 1)
                high(r)
            first = Img(0, 0, 0, "first")
            for tc in range(T):
                high(2 * T + tc)
            for half in range(2):
                prep(first, first, 0, 0, half)

            def lw_copy(im, k, j):
                n = pairs_before(k) + j
                if im.kind == "first" and n < pairs_before(k + 1):
                    act.wait_ge(lwt_ready, n + 1)
                    flat = lw[:].rearrange("p a b c -> p (a b c)")
                    nc.scalar.activation(flat[:, n * PAIR_COLS:(n + 1) * PAIR_COLS], bc[:, TOK:TOK + PAIR_COLS],
                                         ACT.Copy).then_inc(lw_ready, 1)

            def square(im, q, o):
                k = LN[q]
                layer, _, par = PHASES[k]
                act.wait_ge(h_ready, at(im, NPH * BANKS, k * BANKS + o // OPB + 1))
                again = not (im.kind == "first" and q == 0)
                if o == 0:
                    place = sqsum
                    if q > 0:
                        act.wait_ge(small_used, small_no(im, f"ln{q - 1}") + 1)
                    elif again:
                        act.wait_ge(small_used, small_no(im, "ln0") - len(NEXT))
                elif o == 4:
                    place = rstd_all
                    if again:
                        act.wait_ge(t_ready, at(im, T * len(LN), T * q))
                else:
                    place = sq
                    if o > 1 or again:
                        act.wait_ge(sq_used, at(im, 5 * len(LN), 5 * q + {1: 0, 2: 1, 3: 2, 5: 3}[o]))
                nc.scalar.activation(place[:], h[par][:, o, :], ACT.Square, bias=bias[layer][:, o:o + 1],
                                     scale=1.0).then_inc(sq_ready, 1)

            def spread(im, q):
                act.wait_ge(bc_ready, at(im, len(LN), q + 1))
                nc.scalar.activation(rstd_all[:], bc[:, 0:TOK], ACT.Copy).then_inc(rb_ready, 1)

            def gelu(im, q, o):
                k = LN[q]
                layer = PHASES[k][0]
                act.wait_ge(t_ready, at(im, T * len(LN), T * q + o + 1))
                t = t_ring[:, o % RING, :]
                nc.scalar.activation(t, t, ACT.Gelu, bias=bet[layer][:, o:o + 1], scale=gam[layer][:, o:o + 1]) \
                    .then_inc(act_ready, 1)

            def phase(im, k):
                prev = LN.index(k - 1) if k - 1 in LN else None
                this = LN.index(k) if k in LN else None
                if prev is not None:
                    square(im, prev, 4)
                    square(im, prev, 5)
                if k == 0:
                    prep(im, im, 1, 1, 0)
                    prep(im, im, 1, 1, 1)
                if k in (5, 6):
                    prep(im, im, k - 3, k + 1, 0)
                    prep(im, im, k - 3, k + 1, 1)
                if k == NPH - 1 and im.kind != "last":
                    prep(im, after(im), 0, NPH, 0)
                    prep(im, after(im), 0, NPH, 1)
                if this is not None:
                    square(im, this, 0)
                    square(im, this, 1)
                if prev is not None:
                    spread(im, prev)
                    for o in range(3):
                        gelu(im, prev, o)
                if this is not None:
                    square(im, this, 2)
                for o in range(3, T):
                    if prev is not None:
                        lw_copy(im, k, o - 3)
                        gelu(im, prev, o)
                    if this is not None and o == 4:
                        square(im, this, 3)
                for j in range(3 if prev is not None else 0, len(AT_LW)):
                    lw_copy(im, k, j)

            def image(im):
                for k in range(NPH):
                    phase(im, k)

            images(act, image, image, image)

        @block.gpsimd
        def _(pool):
            nc.gpsimd.memset(mhalf, -0.5).then_inc(const_ready, 1)
            nc.gpsimd.memset(sq[:, 0:P], 1.0).then_inc(const_ready, 1)
            nc.gpsimd.memset(ident[:], 0.0).then_inc(const_ready, 1)
            nc.gpsimd.memset(gmean[:], 1.0 / PPG).then_inc(const_ready, 1)
            pool.wait_ge(const_ready, 4)
            nc.gpsimd.tensor_copy(ones_r[:], sq[:, 0:P]).then_inc(const_ready, 1)
            nc.gpsimd.affine_select(out=ident[:], in_=ident[:], compare_op=ALU.not_equal, fill=1.0, base=0,
                                    pattern=[[-1, P]], channel_multiplier=1).then_inc(const_ready, 1)
            groups = gmean[:].rearrange("p (g r) -> p g r", r=PPG)
            nc.gpsimd.affine_select(out=groups, in_=groups, compare_op=ALU.is_ge, fill=0.0, base=0,
                                    pattern=[[-PPG, P // PPG], [0, PPG]], channel_multiplier=1).then_inc(gm_ready, 1)
            pool.wait_ge(gm_ready, 1)
            nc.gpsimd.affine_select(out=groups, in_=groups, compare_op=ALU.is_ge, fill=0.0, base=PPG - 1,
                                    pattern=[[PPG, P // PPG], [0, PPG]], channel_multiplier=-1).then_inc(const_ready, 1)

            def group_rstd(n, which):
                pool.wait_ge(small_used, n + 1)
                nc.gpsimd.tensor_tensor(gs[:, which, 6:7], gs[:, which, 5:6], mhalf[:, 0:1], ALU.pow) \
                    .then_inc(grstd_ready, 1)

            def add(im, q, n):
                value = at(im, T * len(LN), T * q + n + 2)
                pool.wait_ge(sq_ready, value)
                if n > 0:
                    pool.wait_ge(sq_used, at(im, 5 * len(LN), 5 * q + n))
                plane = rstd_all if n + 1 == 4 else sq
                nc.gpsimd.tensor_tensor(sqsum[:], sqsum[:], plane[:], ALU.add).then_inc(sq_used, 1)

            def ln_rstd(im, q):
                pool.wait_ge(small_used, small_no(im, f"ln{q}") + 1)
                nc.gpsimd.tensor_tensor(lnr, lnv, mhalf, ALU.pow).then_inc(rstd_ready, 1)

            def image(im):
                for k in range(NPH):
                    prev = LN.index(k - 1) if k - 1 in LN else None
                    this = LN.index(k) if k in LN else None
                    if prev is not None:
                        add(im, prev, 3)
                        add(im, prev, 4)
                        ln_rstd(im, prev)
                    if this is not None:
                        add(im, this, 0)
                    if k == 1 and im.kind != "first":
                        group_rstd(small_no(im, "g2"), 1)
                    if k == 10 and im.kind != "last":
                        group_rstd(small_no(im, "gx2"), 0)
                    if this is not None:
                        add(im, this, 1)
                        add(im, this, 2)

            group_rstd(3, 0)
            images(pool, image, image, image)
            group_rstd(small_no(end, "g2"), 1)

        @block.vector
        def _(dve):
            dve.wait_ge(vec_loaded, 8 * 16)
            for m in range(2):
                nc.vector.reduce_sum(wmean[:, 2 * T + m:2 * T + m + 1], bias[m], AX.X).then_inc(wstep, 1)

            def minus_mean(r):
                dve.wait_ge(wsum_ready, r + 1)
                nc.vector.tensor_scalar(wmean[:, r:r + 1], wmean[:, r:r + 1], -1.0 / C, None, ALU.mult) \
                    .then_inc(wmean_ready, 1)

            def low(r):
                m, tc = r // T, r % T
                hi = w_hi[:, m, tc, :, :].rearrange("p a b -> p (a b)").bitcast(F32)
                lo = w_lo[:, m, tc, :, :].rearrange("p a b -> p (a b)")
                dve.wait_ge(whi_ready, r + 1)
                if m < 2:
                    nc.vector.scalar_tensor_tensor(out=lo, in0=wt_row(r), scalar=wmean[:, r:r + 1], in1=hi,
                                                   op0=ALU.add, op1=ALU.subtract).then_inc(wt_used, 1)
                else:
                    nc.vector.tensor_tensor(lo, wt_row(r), hi, ALU.subtract).then_inc(wt_used, 1)

            def centre_bias(m):
                mean = wmean[:, 2 * T + 2 + m:2 * T + 3 + m]
                dve.wait_ge(small_ready, m + 1)
                nc.vector.tensor_scalar(mean, small[:, 0:1], -1.0 / C, None, ALU.mult).then_inc(small_used, 1)
                dve.wait_ge(small_used, m + 1)
                nc.vector.tensor_scalar(bias[m], bias[m], mean, None, ALU.add).then_inc(wstep, 1)

            def x_stats(im, n):
                t, piece = n // (HW // XCH), n % (HW // XCH)
                dve.wait_ge(x_loaded[im.slot], (im.use + 1) * 32)
                nc.vector.bn_stats(xstat[:, n, :], x_sb[:, im.slot, t, piece * XCH:(piece + 1) * XCH]) \
                    .then_inc(xstat_ready, 1)

            def gn_mean(im, which, name):
                if which == 0:
                    dve.wait_ge(xstat_ready, (im.i + 2) * len(XPIECES))
                    dve.nop(nofuse=True)
                    stat = xstat[:].rearrange("p a b -> p (a b)")
                else:
                    dve.wait_ge(ystat_ready, im.i * T * TILES)
                    dve.nop(nofuse=True)
                    for t in range(T):
                        nc.vector.bn_aggr(ymean[:, t, :], ystat[:, t, :, :].rearrange("p a b -> p (a b)"))
                    stat = ystat[:].rearrange("p t a b -> p (t a b)")
                nc.vector.bn_aggr(gs[:, which, 0:2], stat).then_inc(step, 1)

            def gn_spread(im, which, n, name):
                mean, var, gmean_, dev, spread_ = (gs[:, which, c:c + 1] for c in range(5))
                dve.wait_ge(small_ready, n + 1)
                nc.vector.tensor_copy(gmean_, small[:, 0:1])
                nc.vector.tensor_tensor(dev, mean, small[:, 0:1], ALU.subtract).then_inc(small_used, 1)
                dve.wait_ge(small_used, n + 1)
                nc.vector.scalar_tensor_tensor(out=spread_, in0=dev, scalar=dev, in1=var, op0=ALU.mult,
                                               op1=ALU.add).then_inc(step, 1)

            def gn_var(im, which, n):
                dve.wait_ge(small_ready, n + 1)
                nc.vector.tensor_scalar(gs[:, which, 5:6], small[:, 0:1], EPS_GN, None, ALU.add) \
                    .then_inc(small_used, 1)

            def gn_shift(count):
                dve.wait_ge(grstd_ready, count)
                nc.vector.scalar_tensor_tensor(out=gs[:, 0, 7:8], in0=gs[:, 0, 2:3], scalar=-1.0, in1=gs[:, 0, 6:7],
                                               op0=ALU.mult, op1=ALU.mult).then_inc(gx_ready, 1)

            def squeeze_input(im):
                dve.wait_ge(grstd_ready, 2 * im.i + (im.kind != "end"))
                nc.vector.tensor_scalar(se[:, 0, :], ymean[:, :, 0], gs[:, 1, 2:3], gs[:, 1, 6:7],
                                        ALU.subtract, ALU.mult).then_inc(xse_ready, 1)

            def squeeze(im, n, inputs=range(T)):
                planes = squeeze_planes(im, n)
                cols = slice(planes.start * P, planes.stop * P)
                count = at(im, HALVES * T, (n - HALVES) * T)
                for tc in inputs:
                    w = lw[:, tc, :, :].rearrange("p a b -> p (a b)")[:, cols]
                    if tc == 0:
                        dve.wait_ge(xse_ready, im.i)
                        last = im.i * NPH * T if im.kind == "end" else at(im, NPH * T, (3 + n) * T)
                        dve.wait_ge(split_ready, last)
                        nc.vector.tensor_scalar(sacc[:, cols], w, se[:, 0, tc:tc + 1], None, ALU.mult) \
                            .then_inc(sacc_ready, 1)
                    else:
                        dve.wait_ge(sacc_ready, count + tc)
                        nc.vector.scalar_tensor_tensor(out=sacc[:, cols], in0=w, scalar=se[:, 0, tc:tc + 1],
                                                       in1=sacc[:, cols], op0=ALU.mult, op1=ALU.add) \
                            .then_inc(sacc_ready, 1)

            def squeeze_bias(im, n):
                no, half = small_no(im, f"se{n}"), slice(n * T // HALVES, (n + 1) * T // HALVES)
                if im.kind == "end":
                    half = slice(0, T)
                dve.wait_ge(small_ready, no + 1)
                nc.vector.tensor_tensor(se[:, 1, half], small[:, 0:half.stop - half.start], lbias[:, half], ALU.add) \
                    .then_inc(small_used, 1)

            def gate(im):
                z, gain, shift = se[:, 1, :], se[:, 2, :], se[:, 3, :]
                dve.wait_ge(small_used, small_no(im, "se0" if im.kind == "end" else "se1") + 1)
                nc.vector.tensor_scalar(z, z, 1.0 / 6.0, 0.5, ALU.mult, ALU.add).then_inc(step, 1)
                dve.wait_ge(step, step_no(im, "z"))
                nc.vector.tensor_scalar(z, z, 0.0, 1.0, ALU.max, ALU.min).then_inc(step, 1)
                dve.wait_ge(step, step_no(im, "gate"))
                nc.vector.tensor_scalar(z, z, gs[:, 1, 6:7], None, ALU.mult).then_inc(step, 1)
                dve.wait_ge(step, step_no(im, "gain"))
                nc.vector.tensor_scalar(gain, z, 1.0, None, ALU.add)
                nc.vector.tensor_scalar(shift, z, gs[:, 1, 2:3], -1.0, ALU.mult, ALU.mult).then_inc(step, 1)
                dve.wait_ge(step, step_no(im, "shift"))

            def excite(im, planes):
                for o in planes:
                    plane = x_sb[:, before(im).slot, o, :]
                    nc.vector.tensor_scalar(plane, plane, se[:, 2, o:o + 1], se[:, 3, o:o + 1], ALU.mult, ALU.add) \
                        .then_inc(out_ready, 1)

            def ln_var(im, q):
                dve.wait_ge(small_ready, small_no(im, f"ln{q}") + 1)
                nc.vector.tensor_scalar(lnv, small[:, 0:2], 1.0 / C, EPS_LN, ALU.mult, ALU.add) \
                    .then_inc(small_used, 1)

            def ln_diag(im, q):
                dve.wait_ge(rstd_ready, at(im, len(LN), q + 1))
                nc.vector.tensor_copy(lnr_hi[:], lnr).then_inc(rhi_ready, 1)
                dve.wait_ge(rhi_ready, at(im, len(LN), q + 1))
                nc.vector.tensor_tensor(lnr_lo[:], lnr, lnr_hi[:].bitcast(F32), ALU.subtract).then_inc(rlo_ready, 1)
                for part, r in enumerate((lnr_hi, lnr_lo)):
                    if part == 1:
                        dve.wait_ge(rlo_ready, at(im, len(LN), q + 1))
                        dve.wait_ge(diag_used, at(im, len(LN), q + 1))
                    nc.vector.tensor_tensor(diag[:].rearrange("p (a b) -> p a b", a=2),
                                            ident[:].unsqueeze(1).to_broadcast([P, 2, P]),
                                            r[:].bitcast(F32).unsqueeze(2).to_broadcast([P, 2, P]), ALU.mult) \
                        .then_inc(diag_ready, 1)

            def normalise(im, q, o):
                layer, _, par = PHASES[LN[q]]
                if o == 0:
                    dve.wait_ge(rb_ready, at(im, len(LN), q + 1))
                dve.wait_ge(split_ready, at(im, NPH * T, (LN[q] + 2) * T + o - RING + 1))
                nc.vector.scalar_tensor_tensor(out=t_ring[:, o % RING, :], in0=h[par][:, o, :],
                                               scalar=bias[layer][:, o:o + 1], in1=rstd_all[:],
                                               op0=ALU.add, op1=ALU.mult).then_inc(t_ready, 1)

            def split(im, k, o, n, between=None):
                par = PHASES[k % NPH][2]
                src = t_ring[:, o % RING:o % RING + n, :]
                hi, lo = a_hi[:, par, o:o + n, :], a_lo[:, par, o:o + n, :]
                dve.wait_ge(act_ready, at(im, NPH * T, k * T + o + n))
                nc.vector.tensor_copy(hi, src).then_inc(hi_ready, n)
                if between:
                    between()
                dve.wait_ge(hi_ready, at(im, NPH * T, k * T + o + n))
                nc.vector.tensor_tensor(lo, src, hi.bitcast(F32), ALU.subtract).then_inc(split_ready, n)

            def x1(im, tile, o, by_bank=False):
                k = [p[:2] for p in PHASES].index((LAYERS - 1, tile))
                xs = x_sb[:, im.slot, o, tile * TOK:(tile + 1) * TOK]
                if by_bank:
                    dve.wait_ge(h_ready, at(im, NPH * BANKS, k * BANKS + o // OPB + 1))
                elif o == 0:
                    dve.wait_ge(h_ready, at(im, NPH * BANKS, (k + 1) * BANKS))
                nc.vector.scalar_tensor_tensor(out=xs, in0=h[PHASES[k][2]][:, o, :], scalar=bias[2][:, o:o + 1], in1=xs,
                                               op0=ALU.add, op1=ALU.add).then_inc(x1_ready, 1)

            def y_stats(im, tile, o):
                dve.wait_ge(x1_ready, at(im, T * TILES, T * tile + o + 1))
                nc.vector.bn_stats(ystat[:, o, tile, :], x_sb[:, im.slot, o, tile * TOK:(tile + 1) * TOK]) \
                    .then_inc(ystat_ready, 1)

            def finish_tile(im, tile, after_planes, by_bank=False):
                for o in range(T):
                    x1(im, tile, o, by_bank)
                    if o >= 1:
                        y_stats(im, tile, o - 1)
                    for f in after_planes.get(o, ()):
                        f()
                y_stats(im, tile, T - 1)

            def phase(im, k):
                prev, nxt = im.kind != "first", im.kind != "last"
                if k - 1 in LN:
                    q = LN.index(k - 1)
                    if k in (2, 3) and prev:
                        squeeze(im, k - 2, range(0, T - 1))
                    if k in X_STATS and nxt:
                        for n in X_STATS[k][0]:
                            x_stats(after(im), n)
                    ln_var(im, q)
                    if k in (2, 3) and prev:
                        squeeze(im, k - 2, range(T - 1, T))
                    if k in X_STATS and nxt:
                        for n in X_STATS[k][1]:
                            x_stats(after(im), n)
                    if k == 1 and prev:
                        gn_spread(im, 1, small_no(im, "g1"), "y")
                    if k == 10 and nxt:
                        gn_spread(im, 0, small_no(im, "gx1"), "x")
                    ln_diag(im, q)
                    if k in (2, 3) and prev:
                        squeeze_bias(im, k - 2)
                    for o in range(RING):
                        normalise(im, q, o)
                    for o in range(T):
                        ahead = o + RING - 1
                        split(im, k + 1, o, 1, (lambda: normalise(im, q, ahead)) if RING <= ahead < T else None)
                        if o == 1 and k == 1 and prev:
                            gn_var(im, 1, small_no(im, "g2"))
                        if o == 1 and k == 10 and nxt:
                            gn_var(im, 0, small_no(im, "gx2"))
                    if k == 1 and prev:
                        squeeze_input(im)
                    if k == 3 and prev:
                        gate(im)
                    if k == 4 and prev:
                        excite(im, range(0, T // 2))
                    if k in X_STATS and nxt:
                        for n in X_STATS[k][2]:
                            x_stats(after(im), n)
                    if k == 9 and nxt:
                        gn_mean(im, 0, "x")
                    if k == 10 and nxt:
                        gn_shift(2 * im.i + 2)
                elif k == 0 and im.kind == "first":
                    for half in range(2):
                        split(im, 1, 3 * half, 3)
                elif k == NPH - 1 and im.kind == "last":
                    finish_tile(im, 2, {})
                else:
                    src, tile = (before(im), TILES - 1) if k == 0 else (im, PHASES[k - 1][1])
                    finish_tile(src, tile, {3: [lambda: split(im, k + 1, 0, 3)], 4: [lambda: split(im, k + 1, 3, 3)]})
                    if k == 0:
                        gn_mean(im, 1, "y")
                    if k == 6 and not prev:
                        dve.wait_ge(lw_ready, LW_PAIRS)
                    if k == 5 and prev:
                        excite(im, range(T // 2, T))

            def image(im):
                for k in range(NPH):
                    phase(im, k)

            first = Img(0, 0, 0, "first")
            stats = 0
            for r in range(3 * T):
                if r < 2 * T:
                    minus_mean(r)
                pieces = 0 if r < FIRST_STATS else 1 if r < 2 * T else 3
                for n in range(stats, min(stats + pieces, len(XPIECES))):
                    x_stats(first, n)
                    stats = n + 1
                if r == 3 * T - 4:
                    gn_mean(setup, 0, "x")
                if r == 3 * T - 3:
                    gn_spread(setup, 0, 2, "x")
                if r == 3 * T - 2:
                    gn_var(setup, 0, 3)
                if r == 3 * T - 1:
                    gn_shift(1)
                low(r)
                if r + 1 in (T, 2 * T):
                    centre_bias(r // T)
            for half in range(2):
                split(first, 0, 3 * half, 3)
            images(dve, image, image, image)
            finish_tile(Img(B - 1, 1, (B - 2) // 2, "last"), TILES - 1, {}, by_bank=True)
            gn_mean(end, 1, "y")
            gn_spread(end, 1, small_no(end, "g1"), "y")
            gn_var(end, 1, small_no(end, "g2"))
            squeeze_input(end)
            squeeze(end, 0)
            squeeze_bias(end, 0)
            gate(end)
            excite(end, range(T))


_INS = ["x", "L0_conv_W1", "L0_conv_b1", "L0_conv_g1", "L0_conv_beta1", "L0_conv_W2", "L0_conv_b2", "L0_conv_g2",
        "L0_conv_beta2", "L0_conv_W3", "L0_conv_b3", "L1_conv_W", "L1_conv_b"]


def kernel(**inputs):
    import numpy as _np
    import concourse.bacc as _bacc
    from concourse import mybir as _mybir
    from concourse.bass_utils import run_bass_kernel_spmd as _run

    nc = _bacc.Bacc("TRN2", target_bir_lowering=False, num_devices=1)
    arrays, args = {}, []
    for name in _INS:
        a = _np.ascontiguousarray(inputs[name])
        arrays[f"in_{name}"] = a
        args.append(nc.dram_tensor(f"in_{name}", a.shape, _mybir.dt.from_np(a.dtype), kind="ExternalInput").ap())
    args.append(nc.dram_tensor("out_0", (B, C, 32, 32), _mybir.dt.float32, kind="ExternalOutput").ap())
    program(nc, *args)
    r = _run(nc, [arrays], core_ids=[0])
    return r.results[0]["out_0"]
```
